# Optimizing a Trainium2 kernel written in Bass

```python
import numpy as np
import jax
import jax.numpy as jnp

def _softmax(x, axis=-1):
    return jax.nn.softmax(x, axis=axis)

def _gelu(x):
    return jax.nn.gelu(x, approximate=True)

def _silu(x):
    return jax.nn.silu(x)

def _sigmoid(x):
    return jax.nn.sigmoid(x)

def _layernorm(x, axis=-1, eps=1e-05):
    m = jnp.mean(x, axis=axis, keepdims=True)
    v = jnp.var(x, axis=axis, keepdims=True)
    return (x - m) / jnp.sqrt(v + eps)

def _scatter_add(tgt, idx, src, axis=0):
    return tgt.at[idx].add(src)

def _segment_sum(src, seg, n):
    return jax.ops.segment_sum(src, seg, n)
kernel_name = 'mk_adj_resnorm_d2_adj_r2_8d173a'

def setup_inputs(seed: int=0):
    np.random.seed(seed)
    _w = jnp.asarray

    def _rec_inputs():
        import jax
        import jax.numpy as jnp
        _gk = jax.random.key(seed)
        x = 7.22e-05 + 1 * jax.random.normal(jax.random.fold_in(_gk, 1), (64, 128, 256), jnp.float32)
        _a = jax.random.bernoulli(jax.random.fold_in(_gk, 2), 0.125, (128, 128))
        _a = jnp.logical_or(_a, jnp.swapaxes(_a, -1, -2))
        _a = jnp.logical_or(_a, jnp.eye(128, dtype=bool))
        adj = _a.astype(jnp.int32)
        return (x, adj)
    x, adj = _rec_inputs()

    def _L0_gnn_setup():
        import jax, jax.numpy as jnp
        import numpy as np
        LEAKY_ALPHA = 0.01
        NEG_INF = -1000000000.0
        LN_EPS = 1e-05

        def _gat_heads(x, adj, W, a):
            O = W.shape[-1]
            Wh = jnp.einsum('bnf,hfo->bhno', x, W)
            f1 = jnp.einsum('bhno,ho->bhn', Wh, a[:, :O])
            f2 = jnp.einsum('bhno,ho->bhn', Wh, a[:, O:])
            e = f1[:, :, :, None] + f2[:, :, None, :]
            e = jnp.where(e > 0, e, LEAKY_ALPHA * e)
            e = jnp.where(adj[None, None] > 0, e, NEG_INF)
            attn = jax.nn.softmax(e, axis=-1)
            return jnp.einsum('bhnm,bhmo->bhno', attn, Wh)
        key = jax.random.key(seed)
        ks = jax.random.split(key, 10)
        B, N, F_in, F_hid, H, F_out, D_ff = (8, 1024, 256, 256, 4, 256, 256)
        s = 0.05
        return {'enc_inputs': jax.random.normal(ks[0], (B, N, F_in), jnp.float32), 'adj': jax.random.randint(ks[1], (N, N), 0, 2, jnp.int32), 'W_heads': jax.random.normal(ks[2], (H, F_in, F_hid), jnp.float32) * s, 'a_heads': jax.random.normal(ks[3], (H, 2 * F_hid), jnp.float32) * s, 'W_out': jax.random.normal(ks[4], (H * F_hid, F_out), jnp.float32) * s, 'a_out': jax.random.normal(ks[5], (2 * F_out,), jnp.float32) * s, 'w1': jax.random.normal(ks[6], (F_out, D_ff), jnp.float32) * s, 'b1': jnp.zeros((D_ff,), jnp.float32), 'w2': jax.random.normal(ks[7], (D_ff, F_out), jnp.float32) * s, 'b2': jnp.zeros((F_out,), jnp.float32), 'ln_gamma': jnp.ones((F_out,), jnp.float32), 'ln_beta': jnp.zeros((F_out,), jnp.float32)}
    _L0_gnn_all = _L0_gnn_setup()
    _L0_gnn_in = {k: v for k, v in _L0_gnn_all.items() if k in ('W_heads', 'a_heads', 'W_out', 'a_out', 'w1', 'b1', 'w2', 'b2', 'ln_gamma', 'ln_beta')}
    del _L0_gnn_all

    def _L1_gnn_setup():
        import jax, jax.numpy as jnp
        import numpy as np
        D_MODEL = 256
        NUM_HEADS = 8
        D_HEAD = D_MODEL // NUM_HEADS
        B, N = (4, 1024)
        key = jax.random.key(seed)
        ks = jax.random.split(key, 10)
        s = 1.0 / np.sqrt(D_MODEL)
        inp = {'h': jax.random.normal(ks[0], (B, N, D_MODEL), dtype=jnp.float32), 'adj': jax.random.randint(ks[1], (N, N), 0, 2, dtype=jnp.int32), 'Wq': jax.random.uniform(ks[2], (D_MODEL, D_MODEL), jnp.float32, -s, s), 'bq': jax.random.uniform(ks[3], (D_MODEL,), jnp.float32, -s, s), 'Wk': jax.random.uniform(ks[4], (D_MODEL, D_MODEL), jnp.float32, -s, s), 'bk': jax.random.uniform(ks[5], (D_MODEL,), jnp.float32, -s, s), 'Wv': jax.random.uniform(ks[6], (D_MODEL, D_MODEL), jnp.float32, -s, s), 'bv': jax.random.uniform(ks[7], (D_MODEL,), jnp.float32, -s, s), 'Wo': jax.random.uniform(ks[8], (D_MODEL, D_MODEL), jnp.float32, -s, s), 'bo': jax.random.uniform(ks[9], (D_MODEL,), jnp.float32, -s, s)}
        return inp
    _L1_gnn_all = _L1_gnn_setup()
    _L1_gnn_in = {k: v for k, v in _L1_gnn_all.items() if k in ('Wq', 'bq', 'Wk', 'bk', 'Wv', 'bv', 'Wo', 'bo')}
    del _L1_gnn_all
    return {'x': x, 'adj': adj, 'L0_gnn_W_heads': _L0_gnn_in['W_heads'], 'L0_gnn_a_heads': _L0_gnn_in['a_heads'], 'L0_gnn_W_out': _L0_gnn_in['W_out'], 'L0_gnn_a_out': _L0_gnn_in['a_out'], 'L0_gnn_w1': _L0_gnn_in['w1'], 'L0_gnn_b1': _L0_gnn_in['b1'], 'L0_gnn_w2': _L0_gnn_in['w2'], 'L0_gnn_b2': _L0_gnn_in['b2'], 'L0_gnn_ln_gamma': _L0_gnn_in['ln_gamma'], 'L0_gnn_ln_beta': _L0_gnn_in['ln_beta'], 'L1_gnn_Wq': _L1_gnn_in['Wq'], 'L1_gnn_bq': _L1_gnn_in['bq'], 'L1_gnn_Wk': _L1_gnn_in['Wk'], 'L1_gnn_bk': _L1_gnn_in['bk'], 'L1_gnn_Wv': _L1_gnn_in['Wv'], 'L1_gnn_bv': _L1_gnn_in['bv'], 'L1_gnn_Wo': _L1_gnn_in['Wo'], 'L1_gnn_bo': _L1_gnn_in['bo']}

def reference(x, adj, L0_gnn_W_heads, L0_gnn_a_heads, L0_gnn_W_out, L0_gnn_a_out, L0_gnn_w1, L0_gnn_b1, L0_gnn_w2, L0_gnn_b2, L0_gnn_ln_gamma, L0_gnn_ln_beta, L1_gnn_Wq, L1_gnn_bq, L1_gnn_Wk, L1_gnn_bk, L1_gnn_Wv, L1_gnn_bv, L1_gnn_Wo, L1_gnn_bo):
    import jax
    import jax.numpy as jnp

    def _L0_gnn_ref(enc_inputs, adj, W_heads, a_heads, W_out, a_out, w1, b1, w2, b2, ln_gamma, ln_beta):
        import jax, jax.numpy as jnp
        import numpy as np
        LEAKY_ALPHA = 0.01
        NEG_INF = -1000000000.0
        LN_EPS = 1e-05

        def _gat_heads(x, adj, W, a):
            O = W.shape[-1]
            Wh = jnp.einsum('bnf,hfo->bhno', x, W)
            f1 = jnp.einsum('bhno,ho->bhn', Wh, a[:, :O])
            f2 = jnp.einsum('bhno,ho->bhn', Wh, a[:, O:])
            e = f1[:, :, :, None] + f2[:, :, None, :]
            e = jnp.where(e > 0, e, LEAKY_ALPHA * e)
            e = jnp.where(adj[None, None] > 0, e, NEG_INF)
            attn = jax.nn.softmax(e, axis=-1)
            return jnp.einsum('bhnm,bhmo->bhno', attn, Wh)
        B, N, _ = enc_inputs.shape
        h = jax.nn.elu(_gat_heads(enc_inputs, adj, W_heads, a_heads))
        h = jnp.transpose(h, (0, 2, 1, 3)).reshape(B, N, -1)
        out = _gat_heads(h, adj, W_out[None], a_out[None])[:, 0]
        out = jax.nn.elu(out)
        ffn = jnp.maximum(out @ w1 + b1, 0.0) @ w2 + b2
        y = ffn + out
        mu = jnp.mean(y, axis=-1, keepdims=True)
        var = jnp.var(y, axis=-1, keepdims=True)
        return (y - mu) / jnp.sqrt(var + LN_EPS) * ln_gamma + ln_beta

    def _L1_gnn_ref(h, adj, Wq, bq, Wk, bk, Wv, bv, Wo, bo):
        import jax, jax.numpy as jnp
        import numpy as np
        D_MODEL = 256
        NUM_HEADS = 8
        D_HEAD = D_MODEL // NUM_HEADS
        B, N = (4, 1024)
        b, n, _ = h.shape

        def split_heads(x):
            return x.reshape(b, n, NUM_HEADS, D_HEAD).transpose(0, 2, 1, 3)
        q = split_heads(h @ Wq.T + bq)
        k = split_heads(h @ Wk.T + bk)
        v = split_heads(h @ Wv.T + bv)
        scale = 1.0 / np.sqrt(D_HEAD)
        scores = jnp.einsum('bhqd,bhkd->bhqk', q, k) * scale
        mask = (adj == 0)[None, None, :, :]
        scores = jnp.where(mask, -jnp.inf, scores)
        attn = jax.nn.softmax(scores, axis=-1)
        out = jnp.einsum('bhqk,bhkd->bhqd', attn, v)
        out = out.transpose(0, 2, 1, 3).reshape(b, n, D_MODEL)
        return out @ Wo.T + bo
    x = _layernorm(x + _L0_gnn_ref(x, adj, L0_gnn_W_heads, L0_gnn_a_heads, L0_gnn_W_out, L0_gnn_a_out, L0_gnn_w1, L0_gnn_b1, L0_gnn_w2, L0_gnn_b2, L0_gnn_ln_gamma, L0_gnn_ln_beta), axis=-1)
    x = _layernorm(x + _L1_gnn_ref(x, adj, L1_gnn_Wq, L1_gnn_bq, L1_gnn_Wk, L1_gnn_bk, L1_gnn_Wv, L1_gnn_bv, L1_gnn_Wo, L1_gnn_bo), axis=-1)
    return x

_drawn_inputs = setup_inputs


def setup_inputs(seed=0):
    import zlib

    import numpy as np

    out = dict(_drawn_inputs(seed))
    spreads = {'L0_gnn_b1': (0.0, 0.1),
     'L0_gnn_b2': (0.0, 0.1),
     'L0_gnn_ln_gamma': (1.0, 0.2),
     'L0_gnn_ln_beta': (0.0, 0.1)}
    factors = {'L1_gnn_Wq': 5.308,
     'L1_gnn_bq': 8.0,
     'L1_gnn_Wk': 5.319,
     'L1_gnn_bk': 8.0,
     'L1_gnn_bv': 2.913}
    for name, (base, spread) in spreads.items():
        noise = np.random.default_rng([zlib.crc32(name.encode()), seed]).standard_normal(out[name].shape)
        drawn = base * np.exp(spread * noise) if base else spread * noise
        out[name] = jnp.asarray(drawn.astype(out[name].dtype))
    for name, factor in factors.items():
        out[name] = (out[name] * factor).astype(out[name].dtype)
    return out
```

```python
from contextlib import ExitStack

import concourse.bass as bass
from concourse import mybir

F32 = mybir.dt.float32
F32R = mybir.dt.float32r
BF16 = mybir.dt.bfloat16
I32 = mybir.dt.int32
ALU = mybir.AluOpType
ACT = mybir.ActivationFunctionType
AX = mybir.AxisListType.X

P = 128
F = 256
KC = F // P
G = 2
HA = 4
O1 = HA * F
K1 = O1 // P
HM = 8
DH = F // HM
RT = P // DH
OB = HM // RT
MASKED = -1e11
SLOPE = 0.01
EPS = 1e-5
LAGS = {"A": 0, "B": 1, "D": 2, "C": 3, "E": 4}
LOW = 32

PRODUCTS = [
    ("x_t", "b4", "A", "x_t_low"), ("ffn1", "b5", "D", "hid_ready"), ("f_t", "b6", "A", "f_t_low"),
    ("qk_scores_0", "d0", "C", "qk_sub_0"), ("qk_scores_1", "d1", "C", "qk_sub_1"), ("ffn2", "b7", "D", "y_ready"),
    ("add_scores_0", "b4", "A", "leaky_0"), ("add_scores_1", "b5", "A", "leaky_1"),
    ("wh2_0", "b6", "B", "wh2_ready_0"), ("wh2_1", "b7", "B", "wh2_ready_1"), ("wh_0", "d0", "A", "wh_ready_0"),
    ("f2_t", "b6", "B", "f2_t_ready"), ("wh_1", "d1", "A", "wh_ready_1"), ("add2_scores", "b7", "B", "leaky2"),
    ("qk_probs_t_0", "d0", "C", "qk_pt_ready_0"), ("qk_probs_t_1", "d1", "C", "qk_pt_ready_1"),
    ("p_t_0", "b5", "A", "p_t_ready_0"), ("p_t_1", "b6", "A", "p_t_ready_1"), ("p2_t", "b4", "B", "p2_t_ready"),
    ("mha_0", "b5", "C", "mha_ready_0"), ("mha_1", "b6", "C", "mha_ready_1"), ("x1_t", "b4", "D", "x1_t_low"),
    ("gat2", "b7", "B", "gat2_ready"), ("gat_0", "d0", "A", "gat_ready_0"), ("gat_1", "d1", "A", "gat_ready_1"),
    ("q", "b4", "D", "q_ready"), ("k", "b7", "D", "k_ready"), ("mha_t", "b5", "C", "mha_t_low"),
    ("v", "b6", "D", "v_ready"), ("proj", "b5", "C", "y2_ready"),
]
PLACE = {product: place for product, place, _, _ in PRODUCTS}


class Count:

    def __init__(self, base, step=0, turn=None):
        self.base, self.step, self.turn = base, step, turn

    def plus(self, n):
        return Count(self.base + n, self.step, self.turn)

    def times(self, n):
        return Count(self.base * n, self.step * n, self.turn)

    def half(self):
        return Count(self.base // 2, self.step // 2, self.turn)

    def value(self):
        return self.base if self.turn is None else self.turn * self.step + self.base


def build(nc, x, adj, W_heads, a_heads, W_out, a_out, w1, b1, w2, b2, ln_gamma, ln_beta,
          WqT, bq, WkT, bk, WvT, bv, WoT, bo, eye, pick, pick2, out):
    NB = x.shape[0]
    NG = NB // G
    FULL = LAGS["E"] + 2
    TURNS = (NG - FULL) // 2
    assert FULL + 2 * TURNS == NG and x.shape[1:] == (P, F)

    x_groups = x.rearrange("(g b) n c -> n g b c", b=G)
    out_groups = out.rearrange("(g b) n c -> n g b c", b=G)

    with ExitStack() as ctx:
        def sb(name, shape, dt=F32):
            return ctx.enter_context(nc.sbuf_tensor(name, shape, dt))

        def parts(name, shape):
            return [sb(name + "_high", shape, F32R), sb(name + "_low", shape, F32R)]

        wh_w = parts("wh_w", [P, KC, O1])
        wf_w = parts("wf_w", [P, KC, P])
        wo_w = parts("wo_w", [P, K1, F + 2])
        w1_w = parts("w1_w", [P, KC, F])
        w2_w = parts("w2_w", [P, KC, F])
        wq_w = parts("wq_w", [P, KC, F])
        wk_w = parts("wk_w", [P, KC, F])
        wv_w = parts("wv_w", [P, KC, F])
        wp_w = parts("wp_w", [P, KC, F])
        ident = sb("ident", [P, P])
        ident_r = sb("ident_r", [P, P], F32R)
        ident_b = sb("ident_b", [P, P], BF16)
        mask4 = sb("mask4", [P, 4, P], BF16)
        pick_r = sb("pick_r", [LOW + 2 * HA, 2 * HA, P], F32R)
        pick2_f = sb("pick2_f", [4, 2, P])
        pick2_r = sb("pick2_r", [4, 2, P], F32R)
        ones = sb("ones", [P, P])
        colsum = sb("colsum", [P, F + 2])
        gamma_r = sb("gamma_r", [P, F])
        beta_r = sb("beta_r", [P, F])
        b2_r = sb("b2_r", [P, F])
        bv_r = sb("bv_r", [P, F])
        bo_r = sb("bo_r", [P, F])
        b1_c = sb("b1_c", [P, KC])
        bq_c = sb("bq_c", [P, OB])
        bk_c = sb("bk_c", [P, OB])
        eps = sb("eps", [P, G])
        power = sb("power", [P, G])

        x_tok = sb("x_tok", [P, 2, G, F])
        x_t = parts("x_t", [P, KC, G, P])
        f_t = sb("f_t", [LOW + 2 * HA, G, P], F32R)
        add_p = sb("add_p", [P, HA, G, P])
        add_max = sb("add_max", [P, HA * G])
        add_sum = sb("add_sum", [P, HA * G])
        add_rec = sb("add_rec", [P, HA * G])
        add_pt = sb("add_pt", [P, HA, G, P])
        wh = sb("wh", [P, G, O1])
        gat_e = sb("gat_e", [P, G, O1])
        gat_g = sb("gat_g", [P, G, O1])
        gat_gp = parts("gat_gp", [P, G, K1, P])
        wh2 = sb("wh2", [P, G, F + 2])
        f2 = sb("f2", [P, G, 4])
        f2_t = sb("f2_t", [4, G, P], F32R)
        add2_p = sb("add2_p", [P, G, P])
        add2_max = sb("add2_max", [P, G])
        add2_sum = sb("add2_sum", [P, G])
        add2_rec = sb("add2_rec", [P, G])
        add2_pt = sb("add2_pt", [P, G, P])
        shared = sb("shared", [P, K1 * (F + 2)])
        gat2_e = shared[:, 0:512].rearrange("p (k b n) -> p k b n", k=KC, b=G)
        gat2_g = shared[:, 512:1024].rearrange("p (k b n) -> p k b n", k=KC, b=G)
        y2 = shared[:, 1024:2048].rearrange("p (a b n) -> p a b n", a=2, b=G)
        gat2_gp = parts("gat2_gp", [P, KC, G, P])
        hid = sb("hid", [P, KC, G, P])
        hid_p = parts("hid_p", [P, KC, G, P])
        y = sb("y", [P, G, F])
        stats = sb("stats", [P, G, 6])
        mv = sb("mv", [P, G, 2])
        vare = sb("vare", [P, G])
        rstd = sb("rstd", [P, G])
        x_res = sb("x_res", [P, 2, G, F])
        xb = sb("xb", [P, G, F])
        stats1 = sb("stats1", [P, G, 6])
        mv1 = sb("mv1", [P, G, 2])
        vare1 = sb("vare1", [P, G])
        rstd1 = sb("rstd1", [P, G])
        x1 = sb("x1", [P, G, F])
        x1b = sb("x1b", [P, 2, G, F])
        x1_t = parts("x1_t", [P, KC, G, P])
        q_s = sb("q_s", [P, OB, G, P])
        k_s = sb("k_s", [P, OB, G, P])
        v_s = sb("v_s", [P, G, HM, DH + 1])
        qk_p = sb("qk_p", [P, RT, OB, G, P])
        qk_max = sb("qk_max", [P, RT, OB * G])
        qk_pt = sb("qk_pt", [P, RT, OB, G, P])
        mha_rec = sb("mha_rec", [P, G, HM])
        mha = sb("mha", [P, G, F])
        mha_t = parts("mha_t", [P, KC, G, P])
        stats2 = sb("stats2", [P, G, 6])
        mv2 = sb("mv2", [P, 2, G, 2])
        vare2 = sb("vare2", [P, G])
        rstd2 = sb("rstd2", [P, G])
        out_s = sb("out_s", [P, 2, G, F])
        stage_w = wh[:].rearrange("p b n -> p (b n)")
        stage_wo = shared[:].rearrange("p (k n) -> p k n", k=K1)
        stage_s = qk_p[:].rearrange("p a b c d -> p (a b c d)")
        stage_s2 = qk_pt[:].rearrange("p a b c d -> p (a b c d)")
        a_r = gat_g[:].rearrange("p b n -> p (b n)")
        prod = gat_e[:].rearrange("p b n -> p (b n)")
        a2_r = x1b[:].rearrange("p a b c -> p (a b c)")
        pick_f = add_p[0:LOW + 2 * HA].rearrange("p h b m -> p (h b) m")
        adj_s = sb("adj_s", [P, P], I32)
        wa = sb("wa", [P, KC, 2 * HA])
        stage_f = sb("stage_f", [P, KC, P])

        small_w = [(w1, w1_w), (w2, w2_w), (WqT, wq_w), (WkT, wk_w), (WvT, wv_w), (WoT, wp_w)]

        def small_stage(i):
            s = stage_s if i < 4 else stage_s2
            i %= 4
            return s[:, i * KC * F:(i + 1) * KC * F].rearrange("p (k n) -> p k n", k=KC)

        bank = {"d0": ctx.enter_context(nc.psum_tensor("d0", [P, 1024], F32)),
                "d1": ctx.enter_context(nc.psum_tensor("d1", [P, 1024], F32))}
        for name in ("b4", "b5", "b6", "b7"):
            bank[name] = ctx.enter_context(nc.psum_tensor(name, [P, 512], F32))

        def at(product):
            return bank[PLACE[product]]

        by_name = {}

        def sems(names):
            new = {n: ctx.enter_context(nc.semaphore(n)) for n in names.split()}
            by_name.update(new)
            return new

        pe_done = sems("x_t_done ffn1_done f_t_done qk_scores_done_0 qk_scores_done_1 ffn2_done add_scores_done_0 "
                    "add_scores_done_1 wh2_done_0 wh2_done_1 wh_done_0 wh_done_1 f2_t_done add2_scores_done "
                    "p2_t_done qk_probs_t_done_0 qk_probs_t_done_1 p_t_done_0 p_t_done_1 x1_t_done gat2_done "
                    "mha_done_0 mha_done_1 gat_done_0 gat_done_1 q_done k_done mha_t_done v_done proj_done")
        act_done = sems("x_t_high hid_ready f_t_high qk_exp_0 qk_exp_1 add_exp wh_ready_0 wh_ready_1 add2_exp "
                     "p2_t_ready qk_pt_ready_0 qk_pt_ready_1 p_t_ready_0 p_t_ready_1 x1_t_high gat2_exp gat2_high "
                     "slope_0 slope_1 slope2 gat_exp_0 gat_exp_1 q_ready k_ready mha_t_high")
        dve_done = sems("x_t_low hid_high hid_low f_t_low qk_max_0 qk_max_1 qk_sub_0 qk_sub_1 y_ready y_stats y_mv "
                     "leaky_0 leaky_1 add_max_ready add_sub y_scaled y_added y1_stats y1_mv wh2_ready_0 wh2_ready_1 "
                     "f2_high f2_low add_sum_ready add_rec_ready add_norm x1_ready f2_t_ready leaky2 "
                     "add2_max_ready add2_sub add2_sum_ready add2_rec_ready add2_norm x1_t_low gat2_ready "
                     "gat2_low mha_rec_0 mha_rec_1 mha_ready_0 mha_ready_1 gat_ready_0 gat_ready_1 gat_high_0 "
                     "gat_high_1 mha_t_low v_ready y2_ready y2_stats y2_mv out_ready")
        pool_done = sems("xb_ready vare_ready rstd_ready vare1_ready rstd1_ready vare2_ready rstd2_ready x1b_ready "
                      "gat_low_0 gat_low_1")
        x_landed = [ctx.enter_context(nc.semaphore(f"x_landed_{i}")) for i in range(2)]
        xres_landed = [ctx.enter_context(nc.semaphore(f"xres_landed_{i}")) for i in range(2)]
        stored = [ctx.enter_context(nc.semaphore(f"stored_{i}")) for i in range(2)]
        big_landed = ctx.enter_context(nc.semaphore("big_landed"))
        small_landed = ctx.enter_context(nc.semaphore("small_landed"))
        set_dve = ctx.enter_context(nc.semaphore("set_dve"))
        set_pe = ctx.enter_context(nc.semaphore("set_pe"))
        set_pool = ctx.enter_context(nc.semaphore("set_pool"))
        weights_ready = ctx.enter_context(nc.semaphore("weights_ready"))

        def flat(t, names):
            return t.rearrange(f"p {names} -> p ({names})")

        block = ctx.enter_context(nc.Block())

        def iterations(eng, body):
            def one(it):
                g = {s: it.plus(-lag) for s, lag in LAGS.items()}
                live = {s for s, c in g.items() if it.turn is not None or 0 <= c.base < NG}
                body(g, live, it)

            for i in range(FULL):
                one(Count(i))
            with eng.Fori(0, TURNS) as turn:
                for u in range(2):
                    one(Count(FULL + u, 2, turn))
            for i in range(NG, NG + LAGS["E"]):
                one(Count(i))

        @block.sync
        def _(sp):
            sp.dma_start(stage_w.rearrange("p (k h o) -> p k h o", k=KC, h=HA)[:, 0],
                         W_heads.rearrange("h (k p) o -> k p h o", k=KC)[0]).then_inc(big_landed, 16)
            sp.dma_start(stage_w.rearrange("p (k h o) -> p k h o", k=KC, h=HA)[:, 1],
                         W_heads.rearrange("h (k p) o -> k p h o", k=KC)[1]).then_inc(big_landed, 16)
            sp.dma_start(a_r, a_heads.rearrange("h o -> (h o)").rearrange("(a o) -> a o", a=1)
                         .broadcast_to([P, 2 * O1])).then_inc(big_landed, 16)
            sp.dma_start(stage_wo[:, :, 0:F], W_out.rearrange("(k p) n -> p k n", p=P)).then_inc(big_landed, 16)
            sp.dma_start(a2_r[:, 0:2 * F], a_out.rearrange("(a o) -> a o", a=1)
                         .broadcast_to([P, 2 * F])).then_inc(big_landed, 16)
            for i, (w, _) in enumerate(small_w):
                sp.dma_start(small_stage(i), w.rearrange("(k p) n -> p k n", p=P)).then_inc(small_landed, 16)

            def body(g, live, it):
                if "A" in live:
                    par = g["A"].base % 2
                    if g["A"].base >= 2:
                        sp.wait_ge(pe_done["x_t_done"], g["A"].plus(-1).value())
                    sp.dma_start(x_tok[:, par], x_groups[:, g["A"].value()]).then_inc(x_landed[par], 16)
                if "B" in live:
                    par = g["B"].base % 2
                    if g["B"].base >= 2:
                        sp.wait_ge(pool_done["xb_ready"], g["B"].plus(-1).value())
                    sp.dma_start(x_res[:, par], x_groups[:, g["B"].value()]).then_inc(xres_landed[par], 16)
                if "E" in live:
                    par = g["E"].base % 2
                    sp.wait_ge(dve_done["out_ready"], g["E"].plus(1).value())
                    sp.dma_start(out_groups[:, g["E"].value()], out_s[:, par]).then_inc(stored[par], 16)

            iterations(sp, body)
            for par in range(2):
                sp.wait_ge(stored[par], 16 * (NG // 2))

        @block.tensor
        def _(pe):
            def read(product, it):
                ring = [p for p in PRODUCTS if p[1] == PLACE[product]]
                here = [p[0] for p in ring].index(product)
                for back in range(1, 8 * len(ring)):
                    _, _, stage, last_read = ring[(here - back) % len(ring)]
                    before = it.plus((here - back) // len(ring) - LAGS[stage])
                    if it.turn is not None or 0 <= before.base < NG:
                        return by_name[last_read], before.plus(1).value()
                return weights_ready, 1

            pe.wait_ge(set_dve, 4)
            for k in range(K1):
                mm = pe.matmul(bank["b4"][:, 0:F + 2], ones[:], stage_wo[:, k, :], start=(k == 0), stop=(k == K1 - 1))
            mm.then_inc(set_pe, 1)
            pe.wait_ge(small_landed, 16 * (len(small_w) + 12))
            for fc in range(KC):
                for oc in range(KC):
                    mm = pe.matmul(bank["b5"][:, fc:fc + 1], small_stage(0)[:, oc, fc * P:(fc + 1) * P],
                                   ones[:, 0:1], start=(oc == 0), stop=(oc == KC - 1))
            mm.then_inc(set_pe, 1)
            pe.wait_ge(weights_ready, 1)

            def split_product(dst, lhs, rhs):
                n = len(lhs[0])
                for k in range(n):
                    for i, (a, b) in enumerate(((0, 0), (0, 1), (1, 0))):
                        mm = pe.matmul(dst, lhs[a][k], rhs[b][k], start=(k == 0 and i == 0),
                                       stop=(k == n - 1 and i == 2))
                return mm

            def chunks(pair, index):
                return [[index(t, k) for k in range(KC)] for t in pair]

            def body(g, live, it):
                A, B, D, C = ("A" in live), ("B" in live), ("D" in live), ("C" in live)
                n_a, n_b, n_d, n_c = [g[stage].plus(1).value() for stage in "ABDC"]

                if A:
                    par = g["A"].base % 2
                    pe.wait_ge(x_landed[par], g["A"].half().plus(1).times(16).value())
                    pe.wait_ge(*read("x_t", it))
                    ps = at("x_t")
                    for kc in range(KC):
                        for b in range(G):
                            mm = pe.transpose(ps[:, (kc * G + b) * P:(kc * G + b + 1) * P],
                                              x_tok[:, par, b, kc * P:(kc + 1) * P], ident[:])
                    mm.then_inc(pe_done["x_t_done"], 1)
                if D:
                    pe.wait_ge(*read("ffn1", it))
                    ps = at("ffn1")
                    pe.wait_ge(act_done["gat2_high"], n_d)
                    pe.wait_ge(dve_done["gat2_low"], n_d)
                    for fc in range(KC):
                        mm = split_product(ps[:, fc * F:(fc + 1) * F],
                                           chunks(w1_w, lambda t, k: t[:, k, fc * P:(fc + 1) * P]),
                                           chunks(gat2_gp, lambda t, k: t[:, k].rearrange("p b n -> p (b n)")))
                    mm.then_inc(pe_done["ffn1_done"], 1)
                if A:
                    pe.wait_ge(*read("f_t", it))
                    ps = at("f_t")
                    pe.wait_ge(act_done["x_t_high"], n_a)
                    pe.wait_ge(dve_done["x_t_low"], n_a)
                    mm = split_product(ps[:, 0:G * P], chunks(wf_w, lambda t, k: t[:, k, :]),
                                       chunks(x_t, lambda t, k: t[:, k].rearrange("p b n -> p (b n)")))
                    mm.then_inc(pe_done["f_t_done"], 1)
                if C:
                    pe.wait_ge(act_done["q_ready"], n_c)
                    pe.wait_ge(act_done["k_ready"], n_c)
                    pe.wait_ge(*read("qk_scores_0", it))
                    pe.wait_ge(*read("qk_scores_1", it))
                    halves = [at("qk_scores_0"), at("qk_scores_1")]
                    tiles = [halves[r // 2][:, (r % 2) * 512:(r % 2 + 1) * 512] for r in range(RT)]
                    for r in range(RT):
                        pe.matmul(tiles[r], ident_b[:], mask4[:].rearrange("p a n -> p (a n)"), start=True, stop=True)
                    for ob in range(OB):
                        for b in range(G):
                            j = ob * G + b
                            for r in range(RT):
                                rows = slice(r * DH, (r + 1) * DH)
                                mm = pe.matmul(tiles[r][:, j * P:(j + 1) * P], q_s[rows, ob, b, :], k_s[rows, ob, b, :],
                                               start=False, stop=True, skip_group_check=True)
                                if j == OB * G - 1 and r == 1:
                                    mm.then_inc(pe_done["qk_scores_done_0"], 1)
                    mm.then_inc(pe_done["qk_scores_done_1"], 1)
                if D:
                    pe.wait_ge(*read("ffn2", it))
                    ps = at("ffn2")
                    pe.wait_ge(dve_done["hid_low"], n_d)
                    for b in range(G):
                        split_product(ps[:, b * F:(b + 1) * F], chunks(hid_p, lambda t, k: t[:, k, b, :]),
                                      chunks(w2_w, lambda t, k: t[:, k, :]))
                        for oc in range(KC):
                            for part in gat2_gp:
                                mm = pe.matmul(ps[:, b * F + oc * P:b * F + (oc + 1) * P], part[:, oc, b, :], ident_r[:],
                                               start=False, stop=(part is gat2_gp[1]),
                                               skip_group_check=True)
                    mm.then_inc(pe_done["ffn2_done"], 1)
                if A:
                    pe.wait_ge(dve_done["f_t_low"], n_a)
                    for hp in range(HA // 2):
                        pe.wait_ge(*read(f"add_scores_{hp}", it))
                        ps = at(f"add_scores_{hp}")
                        by_graph = ps[:].rearrange("p (h b m) -> p b h m", h=2, b=G)
                        pe.matmul(ps[:], ident_b[:], mask4[:].rearrange("p a n -> p (a n)"), start=True, stop=True)
                        for b in range(G):
                            pe.matmul(by_graph[:, b], f_t[:, b, :], pick_r[:, 2 * hp:2 * hp + 2, :],
                                      start=False, stop=False, skip_group_check=True)
                        for h in range(2):
                            mm = pe.matmul(ps[:, h * G * P:(h + 1) * G * P], pick_r[:, HA + 2 * hp + h, :],
                                           f_t[:].rearrange("p b n -> p (b n)"), start=False, stop=True,
                                           skip_group_check=True)
                        mm.then_inc(pe_done[f"add_scores_done_{hp}"], 1)
                if B:
                    for b in range(G):
                        pe.wait_ge(*read(f"wh2_{b}", it))
                        ps = at(f"wh2_{b}")
                        pe.wait_ge(dve_done[f"gat_high_{b}"], n_b)
                        pe.wait_ge(pool_done[f"gat_low_{b}"], n_b)
                        mm = split_product(ps[:, 0:F + 2], [[t[:, b, k, :] for k in range(K1)] for t in gat_gp],
                                           [[t[:, k, :] for k in range(K1)] for t in wo_w])
                        mm.then_inc(pe_done[f"wh2_done_{b}"], 1)

                def wh_product(b):
                    pe.wait_ge(*read(f"wh_{b}", it))
                    ps = at(f"wh_{b}")
                    for half in range(2):
                        cols = slice(half * 512, (half + 1) * 512)
                        mm = split_product(ps[:, cols], chunks(x_t, lambda t, k: t[:, k, b, :]),
                                           chunks(wh_w, lambda t, k: t[:, k, cols]))
                    mm.then_inc(pe_done[f"wh_done_{b}"], 1)

                if A:
                    wh_product(0)
                if B:
                    pe.wait_ge(*read("f2_t", it))
                    ps = at("f2_t")
                    pe.wait_ge(dve_done["f2_low"], n_b)
                    for b in range(G):
                        mm = pe.transpose(ps[0:4, b * P:(b + 1) * P], f2[:, b, :], ident[:])
                    mm.then_inc(pe_done["f2_t_done"], 1)
                if A:
                    wh_product(1)
                if B:
                    pe.wait_ge(*read("add2_scores", it))
                    ps = at("add2_scores")
                    pe.wait_ge(dve_done["f2_t_ready"], n_b)
                    pe.matmul(ps[:, 0:G * P], ident_b[:], mask4[:, 0:G, :].rearrange("p a n -> p (a n)"),
                              start=True, stop=True)
                    for b in range(G):
                        pe.matmul(ps[:, b * P:(b + 1) * P], f2_t[:, b, :], pick2_r[:, 0, :], start=False, stop=False,
                                  skip_group_check=True)
                    pe.matmul(ps[:, 0:G * P], pick2_r[:, 1, :], f2_t[:].rearrange("p b n -> p (b n)"),
                              start=False, stop=True, skip_group_check=True).then_inc(pe_done["add2_scores_done"], 1)
                if C:
                    for half in range(2):
                        pe.wait_ge(*read(f"qk_probs_t_{half}", it))
                        ps = at(f"qk_probs_t_{half}")
                        pe.wait_ge(act_done[f"qk_exp_{half}"], n_c)
                        for r in range(2):
                            for j in range(OB * G):
                                c = (r * OB * G + j) * P
                                mm = pe.transpose(ps[:, c:c + P], qk_p[:, 2 * half + r, j // G, j % G, :], ident[:])
                        mm.then_inc(pe_done[f"qk_probs_t_done_{half}"], 1)
                if A:
                    pe.wait_ge(dve_done["add_norm"], n_a)
                    for hp in range(HA // 2):
                        pe.wait_ge(*read(f"p_t_{hp}", it))
                        ps = at(f"p_t_{hp}")
                        for h in range(2):
                            for b in range(G):
                                c = (h * G + b) * P
                                mm = pe.transpose(ps[:, c:c + P], add_p[:, 2 * hp + h, b, :], ident[:])
                        mm.then_inc(pe_done[f"p_t_done_{hp}"], 1)
                if B:
                    pe.wait_ge(*read("p2_t", it))
                    ps = at("p2_t")
                    pe.wait_ge(dve_done["add2_norm"], n_b)
                    for b in range(G):
                        mm = pe.transpose(ps[:, b * P:(b + 1) * P], add2_p[:, b, :], ident[:])
                    mm.then_inc(pe_done["p2_t_done"], 1)
                if C:
                    pe.wait_ge(act_done["qk_pt_ready_1"], n_c)
                    pe.wait_ge(dve_done["v_ready"], n_c)
                    for b in range(G):
                        pe.wait_ge(*read(f"mha_{b}", it))
                        ps = at(f"mha_{b}")
                        for h in range(HM):
                            mm = pe.matmul(ps[:, h * (DH + 1):(h + 1) * (DH + 1)], qk_pt[:, h % RT, h // RT, b, :],
                                           v_s[:, b, h, :], start=True, stop=True)
                        mm.then_inc(pe_done[f"mha_done_{b}"], 1)
                if D:
                    pe.wait_ge(*read("x1_t", it))
                    ps = at("x1_t")
                    pe.wait_ge(dve_done["x1_ready"], n_d)
                    for kc in range(KC):
                        for b in range(G):
                            c = (kc * G + b) * P
                            mm = pe.transpose(ps[:, c:c + P], x1[:, b, kc * P:(kc + 1) * P], ident[:])
                    mm.then_inc(pe_done["x1_t_done"], 1)
                if B:
                    pe.wait_ge(*read("gat2", it))
                    ps = at("gat2")
                    pe.wait_ge(act_done["p2_t_ready"], n_b)
                    for oc in range(KC):
                        for b in range(G):
                            c = (oc * G + b) * P
                            mm = pe.matmul(ps[:, c:c + P], wh2[:, b, oc * P:(oc + 1) * P], add2_pt[:, b, :],
                                           start=True, stop=True)
                    mm.then_inc(pe_done["gat2_done"], 1)
                if A:
                    pe.wait_ge(act_done["p_t_ready_1"], n_a)
                    pe.wait_ge(act_done["wh_ready_1"], n_a)
                    for b in range(G):
                        pe.wait_ge(*read(f"gat_{b}", it))
                        ps = at(f"gat_{b}")
                        for k in range(K1):
                            mm = pe.matmul(ps[:, k * P:(k + 1) * P], wh[:, b, k * P:(k + 1) * P],
                                           add_pt[:, k // KC, b, :], start=True, stop=True)
                        mm.then_inc(pe_done[f"gat_done_{b}"], 1)
                if D:
                    pe.wait_ge(act_done["x1_t_high"], n_d)
                    pe.wait_ge(dve_done["x1_t_low"], n_d)
                    for name, w, done in (("q", wq_w, pe_done["q_done"]), ("k", wk_w, pe_done["k_done"])):
                        pe.wait_ge(*read(name, it))
                        ps = at(name)
                        for ob in range(OB):
                            mm = split_product(ps[:, ob * F:(ob + 1) * F],
                                               chunks(w, lambda t, k: t[:, k, ob * P:(ob + 1) * P]),
                                               chunks(x1_t, lambda t, k: t[:, k].rearrange("p b n -> p (b n)")))
                        mm.then_inc(done, 1)
                if C:
                    pe.wait_ge(*read("mha_t", it))
                    ps = at("mha_t")
                    pe.wait_ge(dve_done["mha_ready_1"], n_c)
                    for kc in range(KC):
                        for b in range(G):
                            c = (kc * G + b) * P
                            mm = pe.transpose(ps[:, c:c + P], mha[:, b, kc * P:(kc + 1) * P], ident[:])
                    mm.then_inc(pe_done["mha_t_done"], 1)
                if D:
                    pe.wait_ge(*read("v", it))
                    ps = at("v")
                    for b in range(G):
                        mm = split_product(ps[:, b * F:(b + 1) * F], chunks(x1_t, lambda t, k: t[:, k, b, :]),
                                           chunks(wv_w, lambda t, k: t[:, k, :]))
                    mm.then_inc(pe_done["v_done"], 1)
                if C:
                    pe.wait_ge(*read("proj", it))
                    ps = at("proj")
                    pe.wait_ge(act_done["mha_t_high"], n_c)
                    pe.wait_ge(dve_done["mha_t_low"], n_c)
                    for b in range(G):
                        mm = split_product(ps[:, b * F:(b + 1) * F], chunks(mha_t, lambda t, k: t[:, k, b, :]),
                                           chunks(wp_w, lambda t, k: t[:, k, :]))
                    mm.then_inc(pe_done["proj_done"], 1)

            iterations(pe, body)

        @block.scalar
        def _(act):
            for dst, src in ((gamma_r, ln_gamma), (beta_r, ln_beta), (b2_r, b2), (bv_r, bv), (bo_r, bo)):
                act.dma_start(dst[:], src.rearrange("(a o) -> a o", a=1).broadcast_to([P, F])).then_inc(small_landed, 16)
            for dst, src in ((b1_c, b1), (bq_c, bq), (bk_c, bk)):
                act.dma_start(dst[:], src).then_inc(small_landed, 16)
            act.dma_start(ident[:], eye).then_inc(small_landed, 16)
            act.dma_start(pick_f, pick).then_inc(small_landed, 16)
            act.dma_start(pick2_f[:], pick2).then_inc(small_landed, 16)
            act.dma_start(adj_s[:], adj).then_inc(small_landed, 16)
            act.wait_ge(weights_ready, 1)

            def body(g, live, it):
                A, B, D, C = ("A" in live), ("B" in live), ("D" in live), ("C" in live)
                n_a, n_b, n_d, n_c = [g[stage].plus(1).value() for stage in "ABDC"]
                if A:
                    act.wait_ge(pe_done["x_t_done"], n_a)
                    act.activation(x_t[0][:].rearrange("p k b n -> p (k b n)"), at("x_t")[:], ACT.Copy)\
                        .then_inc(act_done["x_t_high"], 1)
                if D:
                    act.wait_ge(pe_done["ffn1_done"], n_d)
                    for fc in range(KC):
                        a = act.activation(hid[:, fc].rearrange("p b n -> p (b n)"), at("ffn1")[:, fc * F:(fc + 1) * F],
                                           ACT.Relu, bias=b1_c[:, fc:fc + 1])
                    a.then_inc(act_done["hid_ready"], 1)
                if A:
                    act.wait_ge(pe_done["f_t_done"], n_a)
                    act.activation(f_t[:].rearrange("p b n -> p (b n)"), at("f_t")[0:LOW + 2 * HA, 0:G * P], ACT.Copy)\
                        .then_inc(act_done["f_t_high"], 1)
                if C:
                    for half in range(2):
                        act.wait_ge(dve_done[f"qk_sub_{half}"], n_c)
                        t = qk_p[:, 2 * half:2 * half + 2].rearrange("p r o b m -> p (r o b m)")
                        act.activation(t, t, ACT.Exp, scale=float(DH) ** -0.5).then_inc(act_done[f"qk_exp_{half}"], 1)
                if A:
                    for hp in range(HA // 2):
                        act.wait_ge(pe_done[f"add_scores_done_{hp}"], n_a)
                        act.activation(flat(add_p[:, 2 * hp:2 * hp + 2], "h b m"), at(f"add_scores_{hp}")[:], ACT.Copy,
                                       scale=SLOPE).then_inc(act_done[f"slope_{hp}"], 1)
                if A:
                    act.wait_ge(dve_done["add_sub"], n_a)
                    t = add_p[:].rearrange("p h b m -> p (h b m)")
                    act.activation(t, t, ACT.Exp).then_inc(act_done["add_exp"], 1)

                def wh_copy(b):
                    act.wait_ge(pe_done[f"wh_done_{b}"], n_a)
                    a = act.activation(wh[:, b, :], at(f"wh_{b}")[:], ACT.Copy, bias=1.0)
                    a.then_inc(act_done[f"wh_ready_{b}"], 1)

                if A:
                    wh_copy(0)
                    wh_copy(1)
                if B:
                    act.wait_ge(pe_done["add2_scores_done"], n_b)
                    act.activation(flat(add2_p[:], "b m"), at("add2_scores")[:, 0:G * P], ACT.Copy, scale=SLOPE)\
                        .then_inc(act_done["slope2"], 1)
                    act.wait_ge(dve_done["add2_sub"], n_b)
                    t = add2_p[:].rearrange("p b m -> p (b m)")
                    act.activation(t, t, ACT.Exp).then_inc(act_done["add2_exp"], 1)
                if C:
                    for half in range(2):
                        act.wait_ge(pe_done[f"qk_probs_t_done_{half}"], n_c)
                        act.activation(qk_pt[:, 2 * half:2 * half + 2].rearrange("p r o b m -> p (r o b m)"),
                                       at(f"qk_probs_t_{half}")[:], ACT.Copy)\
                            .then_inc(act_done[f"qk_pt_ready_{half}"], 1)
                if A:
                    for hp in range(2):
                        act.wait_ge(pe_done[f"p_t_done_{hp}"], n_a)
                        act.activation(add_pt[:, 2 * hp:2 * hp + 2].rearrange("p h b m -> p (h b m)"),
                                       at(f"p_t_{hp}")[:], ACT.Copy)\
                            .then_inc(act_done[f"p_t_ready_{hp}"], 1)
                if B:
                    act.wait_ge(pe_done["p2_t_done"], n_b)
                    act.activation(add2_pt[:].rearrange("p b n -> p (b n)"), at("p2_t")[:, 0:G * P], ACT.Copy)\
                        .then_inc(act_done["p2_t_ready"], 1)
                if D:
                    act.wait_ge(pe_done["x1_t_done"], n_d)
                    act.activation(x1_t[0][:].rearrange("p k b n -> p (k b n)"), at("x1_t")[:], ACT.Copy)\
                        .then_inc(act_done["x1_t_high"], 1)
                if B:
                    act.wait_ge(pe_done["gat2_done"], n_b)
                    act.activation(gat2_e.rearrange("p k b n -> p (k b n)"), at("gat2")[:], ACT.Exp,
                                   bias=-1.0).then_inc(act_done["gat2_exp"], 1)
                if A:
                    act.wait_ge(pe_done["gat_done_0"], n_a)
                    act.activation(gat_e[:, 0, :], at("gat_0")[:], ACT.Exp, bias=-1.0).then_inc(act_done["gat_exp_0"], 1)
                if B:
                    act.wait_ge(dve_done["gat2_ready"], n_b)
                    act.activation(gat2_gp[0][:], gat2_g, ACT.Copy).then_inc(act_done["gat2_high"], 1)
                if A:
                    act.wait_ge(pe_done["gat_done_1"], n_a)
                    act.activation(gat_e[:, 1, :], at("gat_1")[:], ACT.Exp, bias=-1.0).then_inc(act_done["gat_exp_1"], 1)
                if D:
                    for name, dst, bias, done, ready in (("q", q_s, bq_c, pe_done["q_done"], act_done["q_ready"]),
                                                         ("k", k_s, bk_c, pe_done["k_done"], act_done["k_ready"])):
                        act.wait_ge(done, n_d)
                        for ob in range(OB):
                            a = act.activation(dst[:, ob].rearrange("p b n -> p (b n)"), at(name)[:, ob * F:(ob + 1) * F],
                                               ACT.Identity, bias=bias[:, ob:ob + 1])
                        a.then_inc(ready, 1)
                if C:
                    act.wait_ge(pe_done["mha_t_done"], n_c)
                    act.activation(mha_t[0][:].rearrange("p k b n -> p (k b n)"), at("mha_t")[:], ACT.Copy)\
                        .then_inc(act_done["mha_t_high"], 1)

            iterations(act, body)

        @block.gpsimd
        def _(pool):
            pool.memset(ones[:], 1.0).then_inc(set_pool, 1)
            pool.memset(power[:], -0.5).then_inc(set_pool, 1)
            pool.memset(eps[:], EPS).then_inc(set_pool, 1)
            pool.memset(v_s[:], 1.0).then_inc(set_pool, 1)
            pool.memset(stage_f[:], 0.0).then_inc(set_pool, 1)
            pool.wait_ge(weights_ready, 1)

            def inverse_deviation(var, vare, var_ready, vare_ready, rstd, rstd_ready, n):
                pool.wait_ge(var_ready, n)
                pool.tensor_tensor(vare[:], var, eps[:], ALU.add).then_inc(vare_ready, 1)
                pool.wait_ge(vare_ready, n)
                pool.tensor_tensor(rstd[:], vare[:], power[:], ALU.pow).then_inc(rstd_ready, 1)

            def body(g, live, it):
                A, D, C, E = ("A" in live), ("D" in live), ("C" in live), ("E" in live)
                n_a, n_d, n_c, n_e = [g[stage].plus(1).value() for stage in "ADCE"]
                if E:
                    inverse_deviation(mv2[:, g["E"].base % 2, :, 1], vare2, dve_done["y2_mv"], pool_done["vare2_ready"],
                                      rstd2, pool_done["rstd2_ready"], n_e)
                if D:
                    par = g["D"].base % 2
                    pool.wait_ge(xres_landed[par], g["D"].half().plus(1).times(16).value())
                    for b in range(G):
                        p = pool.tensor_tensor(xb[:, b], x_res[:, par, b], beta_r[:], ALU.add)
                    p.then_inc(pool_done["xb_ready"], 1)
                    inverse_deviation(mv[:, :, 1], vare, dve_done["y_mv"], pool_done["vare_ready"], rstd, pool_done["rstd_ready"], n_d)
                    inverse_deviation(mv1[:, :, 1], vare1, dve_done["y1_mv"], pool_done["vare1_ready"], rstd1,
                                      pool_done["rstd1_ready"], n_d)
                    pool.wait_ge(dve_done["x1_ready"], n_d)
                    for b in range(G):
                        p = pool.tensor_tensor(x1b[:, par, b], x1[:, b], bo_r[:], ALU.add)
                    p.then_inc(pool_done["x1b_ready"], 1)
                if A:
                    for b in range(G):
                        pool.wait_ge(dve_done[f"gat_high_{b}"], n_a)
                        pool.tensor_tensor(gat_gp[1][:, b].rearrange("p k n -> p (k n)"), gat_g[:, b, :],
                                           gat_gp[0][:, b].rearrange("p k n -> p (k n)").bitcast(F32), ALU.subtract)\
                            .then_inc(pool_done[f"gat_low_{b}"], 1)

            iterations(pool, body)

        @block.vector
        def _(dve):
            done = [0]

            def then(ins):
                done[0] += 1
                ins.then_inc(set_dve, 1)
                dve.wait_ge(set_dve, done[0])

            def split(pair, src):
                then(dve.tensor_copy(pair[0][:], src))
                dve.tensor_tensor(pair[1][:], src, pair[0][:].bitcast(F32), ALU.subtract)

            dve.wait_ge(big_landed, 16 * 5)
            dve.wait_ge(set_pool, 5)
            for part in range(2):
                prod3 = prod.rearrange("p (k n) -> p k n", k=K1)
                then(dve.tensor_tensor(prod3, stage_wo[:, :, 0:F],
                                       a2_r[:, part * F:(part + 1) * F].unsqueeze(1).broadcast_to([P, K1, F]), ALU.mult))
                then(dve.tensor_reduce(stage_wo[:, :, F + part], prod3, AX, ALU.add))
            split(wo_w, stage_wo)
            for kc in range(KC):
                for part in range(2):
                    pr = prod[:, 0:O1].rearrange("p (h o) -> p h o", h=HA)
                    then(dve.tensor_tensor(pr, stage_w[:, kc * O1:(kc + 1) * O1].rearrange("p (h o) -> p h o", h=HA),
                                           a_r.rearrange("p (h t o) -> p h t o", h=HA, t=2)[:, :, part], ALU.mult))
                    then(dve.tensor_reduce(wa[:, kc, part * HA:(part + 1) * HA], pr, AX, ALU.add))
            then(dve.tensor_copy(stage_f[:, :, 0:2 * HA], wa[:]))
            then(dve.tensor_copy(stage_f[:, :, LOW:LOW + 2 * HA], wa[:]))
            split(wf_w, stage_f[:])
            split(wh_w, stage_w.rearrange("p (k n) -> p k n", k=KC))
            dve.wait_ge(small_landed, 16 * (len(small_w) + 12))
            for i, (_, pair) in enumerate(small_w):
                split(pair, small_stage(i))
            dve.tensor_copy(ident_r[:], ident[:])
            dve.tensor_copy(ident_b[:], ident[:])
            dve.tensor_copy(pick_r[:], pick_f)
            dve.tensor_copy(pick2_r[:], pick2_f[:])
            dve.tensor_scalar(mask4[:], adj_s[:].unsqueeze(1).broadcast_to([P, 4, P]), 0, MASKED, ALU.is_le, ALU.mult)
            dve.wait_ge(set_pe, 1)
            dve.tensor_scalar(colsum[:, 0:F], bank["b4"][:, 0:F], -1.0, None, ALU.add)
            dve.tensor_copy(colsum[:, F:F + 2], bank["b4"][:, F:F + 2])
            dve.wait_ge(set_pe, 2)
            then(dve.tensor_tensor(b1_c[:], b1_c[:], bank["b5"][:, 0:KC], ALU.subtract))
            dve.tensor_scalar(b2_r[:], b2_r[:], -1.0, None, ALU.add)
            dve.memset(add2_max[:], 0.0).then_inc(weights_ready, 1)

            def row_stats(src, stats, ready):
                for b in range(G):
                    d = dve.bn_stats(stats[:, b], src[:, b])
                d.then_inc(ready, 1)

            def mean_variance(mv, stats, ready):
                for b in range(G):
                    d = dve.bn_aggr(mv[:, b], stats[:, b])
                d.then_inc(ready, 1)

            def body(g, live, it):
                A, B, D, C, E = ("A" in live), ("B" in live), ("D" in live), ("C" in live), ("E" in live)
                n_a, n_b, n_d, n_c, n_e = [g[stage].plus(1).value() for stage in "ABDCE"]
                if E:
                    dve.wait_ge(dve_done["y2_stats"], n_e)
                if A:
                    dve.wait_ge(act_done["x_t_high"], n_a)
                    dve.tensor_tensor(flat(x_t[1][:], "k b n"), at("x_t")[:], flat(x_t[0][:], "k b n").bitcast(F32),
                                      ALU.subtract).then_inc(dve_done["x_t_low"], 1)
                if E:
                    mean_variance(mv2[:, g["E"].base % 2], stats2, dve_done["y2_mv"])
                if D:
                    dve.wait_ge(act_done["hid_ready"], n_d)
                    dve.tensor_copy(hid_p[0][:], hid[:]).then_inc(dve_done["hid_high"], 1)
                    dve.wait_ge(dve_done["hid_high"], n_d)
                    dve.tensor_tensor(flat(hid_p[1][:], "k b n"), flat(hid[:], "k b n"),
                                      flat(hid_p[0][:], "k b n").bitcast(F32), ALU.subtract).then_inc(dve_done["hid_low"], 1)
                if A:
                    dve.wait_ge(act_done["f_t_high"], n_a)
                    low = flat(f_t[LOW:LOW + 2 * HA], "b n")
                    dve.tensor_tensor(low, at("f_t")[LOW:LOW + 2 * HA, 0:G * P], low.bitcast(F32), ALU.subtract)\
                        .then_inc(dve_done["f_t_low"], 1)
                if C:
                    for half in range(2):
                        dve.wait_ge(pe_done[f"qk_scores_done_{half}"], n_c)
                        s3 = at(f"qk_scores_{half}")[:].rearrange("p (j m) -> p j m", m=P)
                        mx = flat(qk_max[:, 2 * half:2 * half + 2], "r j")
                        dve.tensor_reduce(mx, s3, AX, ALU.max).then_inc(dve_done[f"qk_max_{half}"], 1)
                        dve.wait_ge(dve_done[f"qk_max_{half}"], n_c)
                        dve.tensor_tensor(qk_p[:, 2 * half:2 * half + 2].rearrange("p r o b m -> p (r o b) m"), s3,
                                          mx.unsqueeze(2).broadcast_to([P, 2 * OB * G, P]), ALU.subtract)\
                            .then_inc(dve_done[f"qk_sub_{half}"], 1)
                if E:
                    par = g["E"].base % 2
                    dve.wait_ge(pool_done["rstd2_ready"], n_e)
                    if g["E"].base >= 2:
                        dve.wait_ge(stored[par], g["E"].half().times(16).value())
                    for b in range(G):
                        d = dve.tensor_scalar(out_s[:, par, b], y2[:, par, b], mv2[:, par, b, 0:1], rstd2[:, b:b + 1],
                                              ALU.subtract, ALU.mult)
                    d.then_inc(dve_done["out_ready"], 1)
                if D:
                    dve.wait_ge(pe_done["ffn2_done"], n_d)
                    dve.tensor_tensor(y[:], at("ffn2")[:].rearrange("p (b n) -> p b n", b=G),
                                      b2_r[:].unsqueeze(1).broadcast_to([P, G, F]), ALU.add).then_inc(dve_done["y_ready"], 1)
                    dve.wait_ge(dve_done["y_ready"], n_d)
                    row_stats(y, stats, dve_done["y_stats"])
                    dve.wait_ge(dve_done["y_stats"], n_d)
                if A:
                    for hp in range(HA // 2):
                        dve.wait_ge(act_done[f"slope_{hp}"], n_a)
                        p2 = flat(add_p[:, 2 * hp:2 * hp + 2], "h b m")
                        dve.tensor_tensor(p2, at(f"add_scores_{hp}")[:], p2, ALU.max)\
                            .then_inc(dve_done[f"leaky_{hp}"], 1)
                        if D and hp == 0:
                            mean_variance(mv, stats, dve_done["y_mv"])
                elif D:
                    mean_variance(mv, stats, dve_done["y_mv"])
                if A:
                    dve.wait_ge(dve_done["leaky_1"], n_a)
                    p3 = add_p[:].rearrange("p h b m -> p (h b) m")
                    dve.tensor_reduce(add_max[:], p3, AX, ALU.max).then_inc(dve_done["add_max_ready"], 1)
                    dve.wait_ge(dve_done["add_max_ready"], n_a)
                    dve.tensor_tensor(p3, p3, add_max[:].unsqueeze(2).broadcast_to([P, HA * G, P]), ALU.subtract)\
                        .then_inc(dve_done["add_sub"], 1)
                if D:
                    dve.wait_ge(pool_done["rstd_ready"], n_d)
                    for b in range(G):
                        d = dve.scalar_tensor_tensor(out=y[:, b], in0=y[:, b], scalar=mv[:, b, 0:1], in1=gamma_r[:],
                                                     op0=ALU.subtract, op1=ALU.mult)
                    d.then_inc(dve_done["y_scaled"], 1)
                    dve.wait_ge(dve_done["y_scaled"], n_d)
                    for b in range(G):
                        d = dve.scalar_tensor_tensor(out=y[:, b], in0=y[:, b], scalar=rstd[:, b:b + 1], in1=xb[:, b],
                                                     op0=ALU.mult, op1=ALU.add)
                    d.then_inc(dve_done["y_added"], 1)
                    dve.wait_ge(dve_done["y_added"], n_d)
                    row_stats(y, stats1, dve_done["y1_stats"])
                    dve.wait_ge(dve_done["y1_stats"], n_d)
                if B:
                    for b in range(G):
                        dve.wait_ge(pe_done[f"wh2_done_{b}"], n_b)
                        dve.tensor_tensor(wh2[:, b], at(f"wh2_{b}")[:, 0:F + 2], colsum[:], ALU.subtract)\
                            .then_inc(dve_done[f"wh2_ready_{b}"], 1)
                        if D and b == 0:
                            mean_variance(mv1, stats1, dve_done["y1_mv"])
                elif D:
                    mean_variance(mv1, stats1, dve_done["y1_mv"])
                if B:
                    dve.wait_ge(dve_done["wh2_ready_1"], n_b)
                    dve.tensor_copy(f2[:, :, 0:2].bitcast(F32R), wh2[:, :, F:F + 2]).then_inc(dve_done["f2_high"], 1)
                    dve.wait_ge(dve_done["f2_high"], n_b)
                    dve.tensor_tensor(f2[:, :, 2:4], wh2[:, :, F:F + 2], f2[:, :, 0:2], ALU.subtract)\
                        .then_inc(dve_done["f2_low"], 1)
                if A:
                    dve.wait_ge(act_done["add_exp"], n_a)
                    p3 = add_p[:].rearrange("p h b m -> p (h b) m")
                    dve.tensor_reduce(add_sum[:], p3, AX, ALU.add).then_inc(dve_done["add_sum_ready"], 1)
                    dve.wait_ge(dve_done["add_sum_ready"], n_a)
                    dve.reciprocal(add_rec[:], add_sum[:]).then_inc(dve_done["add_rec_ready"], 1)
                    dve.wait_ge(dve_done["add_rec_ready"], n_a)
                    dve.tensor_tensor(p3, p3, add_rec[:].unsqueeze(2).broadcast_to([P, HA * G, P]), ALU.mult)\
                        .then_inc(dve_done["add_norm"], 1)
                if D:
                    dve.wait_ge(pool_done["rstd1_ready"], n_d)
                    for b in range(G):
                        d = dve.tensor_scalar(x1[:, b], y[:, b], mv1[:, b, 0:1], rstd1[:, b:b + 1],
                                              ALU.subtract, ALU.mult)
                    d.then_inc(dve_done["x1_ready"], 1)
                if B:
                    dve.wait_ge(pe_done["f2_t_done"], n_b)
                    dve.tensor_copy(flat(f2_t[:], "b n"), at("f2_t")[0:4, 0:G * P]).then_inc(dve_done["f2_t_ready"], 1)
                    dve.wait_ge(act_done["slope2"], n_b)
                    p2 = flat(add2_p[:], "b m")
                    dve.tensor_tensor(p2, at("add2_scores")[:, 0:G * P], p2, ALU.max).then_inc(dve_done["leaky2"], 1)
                    dve.wait_ge(dve_done["leaky2"], n_b)
                    dve.tensor_reduce(add2_max[:], add2_p[:], AX, ALU.max).then_inc(dve_done["add2_max_ready"], 1)
                    dve.wait_ge(dve_done["add2_max_ready"], n_b)
                    dve.tensor_tensor(add2_p[:], add2_p[:], add2_max[:].unsqueeze(2).broadcast_to([P, G, P]),
                                      ALU.subtract).then_inc(dve_done["add2_sub"], 1)
                    dve.wait_ge(act_done["add2_exp"], n_b)
                    dve.tensor_reduce(add2_sum[:], add2_p[:], AX, ALU.add).then_inc(dve_done["add2_sum_ready"], 1)
                    dve.wait_ge(dve_done["add2_sum_ready"], n_b)
                    dve.reciprocal(add2_rec[:], add2_sum[:]).then_inc(dve_done["add2_rec_ready"], 1)
                    dve.wait_ge(dve_done["add2_rec_ready"], n_b)
                    dve.tensor_tensor(add2_p[:], add2_p[:], add2_rec[:].unsqueeze(2).broadcast_to([P, G, P]),
                                      ALU.mult).then_inc(dve_done["add2_norm"], 1)
                if C:
                    for b in range(G):
                        dve.wait_ge(pe_done[f"mha_done_{b}"], n_c)
                        o3 = at(f"mha_{b}")[:, 0:HM * (DH + 1)].rearrange("p (h d) -> p h d", h=HM)
                        dve.reciprocal(mha_rec[:, b], o3[:, :, DH]).then_inc(dve_done[f"mha_rec_{b}"], 1)
                        dve.wait_ge(dve_done[f"mha_rec_{b}"], n_c)
                        dve.tensor_tensor(mha[:, b].rearrange("p (h d) -> p h d", h=HM), o3[:, :, 0:DH],
                                          mha_rec[:, b].unsqueeze(2).broadcast_to([P, HM, DH]), ALU.mult)\
                            .then_inc(dve_done[f"mha_ready_{b}"], 1)
                if D:
                    dve.wait_ge(act_done["x1_t_high"], n_d)
                    dve.tensor_tensor(flat(x1_t[1][:], "k b n"), at("x1_t")[:], flat(x1_t[0][:], "k b n").bitcast(F32),
                                      ALU.subtract).then_inc(dve_done["x1_t_low"], 1)
                if B:
                    dve.wait_ge(act_done["gat2_exp"], n_b)
                    dve.scalar_tensor_tensor(out=flat(gat2_g, "k b n"), in0=flat(gat2_e, "k b n"), scalar=1.0,
                                             in1=at("gat2")[:], op0=ALU.min, op1=ALU.max).then_inc(dve_done["gat2_ready"], 1)

                def gat(b):
                    dve.wait_ge(act_done[f"gat_exp_{b}"], n_a)
                    dve.scalar_tensor_tensor(out=gat_g[:, b], in0=gat_e[:, b], scalar=1.0, in1=at(f"gat_{b}")[:],
                                             op0=ALU.min, op1=ALU.max).then_inc(dve_done[f"gat_ready_{b}"], 1)
                    dve.wait_ge(dve_done[f"gat_ready_{b}"], n_a)
                    dve.tensor_copy(flat(gat_gp[0][:, b], "k n"), gat_g[:, b])\
                        .then_inc(dve_done[f"gat_high_{b}"], 1)

                if A:
                    gat(0)
                if B:
                    dve.wait_ge(act_done["gat2_high"], n_b)
                    dve.tensor_tensor(flat(gat2_gp[1][:], "k b n"), flat(gat2_g, "k b n"),
                                      flat(gat2_gp[0][:], "k b n").bitcast(F32), ALU.subtract).then_inc(dve_done["gat2_low"], 1)
                if A:
                    gat(1)
                if C:
                    dve.wait_ge(act_done["mha_t_high"], n_c)
                    dve.tensor_tensor(flat(mha_t[1][:], "k b n"), at("mha_t")[:], flat(mha_t[0][:], "k b n").bitcast(F32),
                                      ALU.subtract).then_inc(dve_done["mha_t_low"], 1)
                if D:
                    dve.wait_ge(pe_done["v_done"], n_d)
                    dve.tensor_tensor(v_s[:, :, :, 0:DH], at("v")[:].rearrange("p (b h d) -> p b h d", b=G, h=HM),
                                      bv_r[:].rearrange("p (h d) -> p h d", h=HM).unsqueeze(1)
                                      .broadcast_to([P, G, HM, DH]), ALU.add).then_inc(dve_done["v_ready"], 1)
                if C:
                    par = g["C"].base % 2
                    dve.wait_ge(pe_done["proj_done"], n_c)
                    dve.wait_ge(pool_done["x1b_ready"], n_c)
                    dve.tensor_tensor(y2[:, par], at("proj")[:].rearrange("p (b n) -> p b n", b=G), x1b[:, par],
                                      ALU.add).then_inc(dve_done["y2_ready"], 1)
                    dve.wait_ge(dve_done["y2_ready"], n_c)
                    row_stats(y2[:, par], stats2, dve_done["y2_stats"])

            iterations(dve, body)


def kernel(x, adj, L0_gnn_W_heads, L0_gnn_a_heads, L0_gnn_W_out, L0_gnn_a_out, L0_gnn_w1, L0_gnn_b1, L0_gnn_w2,
           L0_gnn_b2, L0_gnn_ln_gamma, L0_gnn_ln_beta, L1_gnn_Wq, L1_gnn_bq, L1_gnn_Wk, L1_gnn_bk, L1_gnn_Wv,
           L1_gnn_bv, L1_gnn_Wo, L1_gnn_bo):
    import numpy as np
    import concourse.bacc as bacc
    from concourse.bass_utils import run_bass_kernel_spmd

    pick = np.zeros((LOW + 2 * HA, 2 * HA, P), np.float32)
    for c in range(2 * HA):
        pick[[c, LOW + c], c] = 1.0
    pick2 = np.zeros((4, 2, P), np.float32)
    for c in range(2):
        pick2[[c, 2 + c], c] = 1.0

    def columns(v):
        return np.asarray(v).reshape(-1, P).T

    arrays = {
        "x": x, "adj": adj, "W_heads": L0_gnn_W_heads, "a_heads": L0_gnn_a_heads, "W_out": L0_gnn_W_out,
        "a_out": L0_gnn_a_out, "w1": L0_gnn_w1, "b1": columns(L0_gnn_b1), "w2": L0_gnn_w2, "b2": L0_gnn_b2,
        "ln_gamma": L0_gnn_ln_gamma, "ln_beta": L0_gnn_ln_beta,
        "WqT": np.asarray(L1_gnn_Wq).T, "bq": columns(L1_gnn_bq), "WkT": np.asarray(L1_gnn_Wk).T, "bk": columns(L1_gnn_bk),
        "WvT": np.asarray(L1_gnn_Wv).T, "bv": L1_gnn_bv, "WoT": np.asarray(L1_gnn_Wo).T, "bo": L1_gnn_bo,
        "eye": np.eye(P, dtype=np.float32), "pick": pick, "pick2": pick2,
    }
    nc = bacc.Bacc("TRN2", target_bir_lowering=False, num_devices=1)
    feeds, args = {}, {}
    for name, a in arrays.items():
        a = np.ascontiguousarray(a)
        feeds[f"in_{name}"] = a
        args[name] = nc.dram_tensor(f"in_{name}", a.shape, mybir.dt.from_np(a.dtype), kind="ExternalInput").ap()
    out = nc.dram_tensor("out_x", tuple(np.shape(x)), F32, kind="ExternalOutput").ap()
    build(nc, out=out, **args)
    return run_bass_kernel_spmd(nc, [feeds], core_ids=[0]).results[0]["out_x"]
```

```python
from contextlib import ExitStack

import concourse.bass as bass
from concourse import mybir

F32 = mybir.dt.float32
F32R = mybir.dt.float32r
BF16 = mybir.dt.bfloat16
I32 = mybir.dt.int32
ALU = mybir.AluOpType
ACT = mybir.ActivationFunctionType
AX = mybir.AxisListType.X

P = 128
F = 256
KC = F // P
G = 2
HA = 4
O1 = HA * F
K1 = O1 // P
HM = 8
DH = F // HM
RT = P // DH
OB = HM // RT
MASKED = -1e11
SLOPE = 0.01
EPS = 1e-5
LAGS = {"X": 0, "A": 1, "B": 2, "D": 3, "C": 4, "E": 5}
LOW = 32

PRODUCTS = [
    ("add_scores_0", "b5", "A", "leaky_0"), ("add_scores_1", "b6", "A", "leaky_1"),
    ("qk_scores_0", "d0", "C", "qk_sub_0"), ("qk_scores_1", "d1", "C", "qk_sub_1"), ("ffn1", "b4", "D", "hid_ready"),
    ("wh2_0", "b5", "B", "wh2_ready_0"), ("ffn2", "b7", "D", "y_ready"), ("wh2_1", "b6", "B", "wh2_ready_1"),
    ("wh_0", "d0", "A", "wh_ready_0"), ("wh_1", "d1", "A", "wh_ready_1"), ("p_t_0", "b4", "A", "p_t_ready_0"),
    ("p_t_1", "b7", "A", "p_t_ready_1"), ("qk_probs_t_0", "d0", "C", "qk_pt_ready_0"),
    ("qk_probs_t_1", "d1", "C", "qk_pt_ready_1"), ("f2_t", "b5", "B", "f2_t_ready"), ("x1_t", "b6", "D", "x1_t_low"),
    ("gat_0", "d0", "A", "gat_ready_0"), ("add2_scores", "b7", "B", "leaky2"), ("mha_0", "b4", "C", "mha_ready_0"),
    ("q", "b6", "D", "q_ready"), ("mha_1", "b5", "C", "mha_ready_1"), ("f_t", "b7", "X", "f_t_low"),
    ("gat_1", "d1", "A", "gat_ready_1"), ("k", "b5", "D", "k_ready"), ("mha_t", "b4", "C", "mha_t_low"),
    ("p2_t", "b7", "B", "p2_t_ready"), ("v", "b6", "D", "v_ready"), ("gat2", "b7", "B", "gat2_ready"),
    ("proj", "b4", "C", "y2_ready"),
]
PLACE = {product: place for product, place, _, _ in PRODUCTS}


class Count:

    def __init__(self, base, step=0, turn=None):
        self.base, self.step, self.turn = base, step, turn

    def plus(self, n):
        return Count(self.base + n, self.step, self.turn)

    def times(self, n):
        return Count(self.base * n, self.step * n, self.turn)

    def half(self):
        return Count(self.base // 2, self.step // 2, self.turn)

    def value(self):
        return self.base if self.turn is None else self.turn * self.step + self.base


def build(nc, x, xT, adj, W_heads, a_heads, W_out, a_out, w1, b1, w2, b2, ln_gamma, ln_beta,
          WqT, bq, WkT, bk, WvT, bv, WoT, bo, eye, pick, pick2, out):
    NB = x.shape[0]
    NG = NB // G
    FULL = LAGS["E"] + 3
    TURNS = (NG - FULL) // 2
    assert FULL + 2 * TURNS == NG and x.shape[1:] == (P, F)

    x_groups = x.rearrange("(g b) n c -> n g b c", b=G)
    out_groups = out.rearrange("(g b) n c -> n g b c", b=G)

    with ExitStack() as ctx:
        def sb(name, shape, dt=F32):
            return ctx.enter_context(nc.sbuf_tensor(name, shape, dt))

        def parts(name, shape):
            return [sb(name + "_high", shape, F32R), sb(name + "_low", shape, F32R)]

        wh_w = parts("wh_w", [P, KC, O1])
        wf_w = parts("wf_w", [P, KC, P])
        wo_w = parts("wo_w", [P, K1, F + 2])
        w1_w = parts("w1_w", [P, KC, F])
        w2_w = parts("w2_w", [P, KC, F])
        wq_w = parts("wq_w", [P, KC, F])
        wk_w = parts("wk_w", [P, KC, F])
        wv_w = parts("wv_w", [P, KC, F])
        wp_w = parts("wp_w", [P, KC, F])
        ident = sb("ident", [P, P])
        ident_r = sb("ident_r", [P, P], F32R)
        ident_b = sb("ident_b", [P, P], BF16)
        mask4 = sb("mask4", [P, 4, P], BF16)
        pick_r = sb("pick_r", [LOW + 2 * HA, 2 * HA, P], F32R)
        pick2_f = sb("pick2_f", [4, 2, P])
        pick2_r = sb("pick2_r", [4, 2, P], F32R)
        ones = sb("ones", [P, P])
        colsum = sb("colsum", [P, F + 2])
        gamma_r = sb("gamma_r", [P, F])
        beta_r = sb("beta_r", [P, F])
        b2_r = sb("b2_r", [P, F])
        bv_r = sb("bv_r", [P, F])
        bo_r = sb("bo_r", [P, F])
        b1_c = sb("b1_c", [P, KC])
        bq_c = sb("bq_c", [P, OB])
        bk_c = sb("bk_c", [P, OB])
        eps = sb("eps", [P, G])
        power = sb("power", [P, G])

        x_in = sb("x_in", [P, 2, KC * G * P])
        x_t = parts("x_t", [P, KC, G, P])
        f_t = sb("f_t", [LOW + 2 * HA, G, P], F32R)
        add_p = sb("add_p", [P, HA, G, P])
        add_max = sb("add_max", [P, HA * G])
        add_sum = sb("add_sum", [P, HA * G])
        add_rec = sb("add_rec", [P, HA * G])
        add_pt = sb("add_pt", [P, HA, G, P])
        wh = sb("wh", [P, G, O1])
        gat_e = sb("gat_e", [P, G, O1])
        gat_g = sb("gat_g", [P, G, O1])
        gat_gp = parts("gat_gp", [P, G, K1, P])
        wh2 = sb("wh2", [P, G, F + 2])
        f2 = sb("f2", [P, G, 4])
        f2_t = sb("f2_t", [4, G, P], F32R)
        add2_p = sb("add2_p", [P, G, P])
        add2_max = sb("add2_max", [P, G])
        add2_sum = sb("add2_sum", [P, G])
        add2_rec = sb("add2_rec", [P, G])
        add2_pt = sb("add2_pt", [P, G, P])
        shared = sb("shared", [P, K1 * (F + 2)])
        gat2_e = shared[:, 0:512].rearrange("p (k b n) -> p k b n", k=KC, b=G)
        gat2_g = shared[:, 512:1024].rearrange("p (k b n) -> p k b n", k=KC, b=G)
        y2 = shared[:, 1024:2048].rearrange("p (a b n) -> p a b n", a=2, b=G)
        gat2_gp = parts("gat2_gp", [P, KC, G, P])
        hid = sb("hid", [P, KC, G, P])
        hid_p = parts("hid_p", [P, KC, G, P])
        y = sb("y", [P, G, F])
        stats = sb("stats", [P, G, 6])
        mv = sb("mv", [P, G, 2])
        vare = sb("vare", [P, G])
        rstd = sb("rstd", [P, G])
        x_res = sb("x_res", [P, 2, G, F])
        xb = sb("xb", [P, G, F])
        stats1 = sb("stats1", [P, G, 6])
        mv1 = sb("mv1", [P, G, 2])
        vare1 = sb("vare1", [P, G])
        rstd1 = sb("rstd1", [P, G])
        x1 = sb("x1", [P, G, F])
        x1b = sb("x1b", [P, 2, G, F])
        x1_t = parts("x1_t", [P, KC, G, P])
        q_s = sb("q_s", [P, OB, G, P])
        k_s = sb("k_s", [P, OB, G, P])
        v_s = sb("v_s", [P, G, HM, DH + 1])
        qk_p = sb("qk_p", [P, RT, OB, G, P])
        qk_max = sb("qk_max", [P, RT, OB * G])
        qk_pt = sb("qk_pt", [P, RT, OB, G, P])
        mha_rec = sb("mha_rec", [P, G, HM])
        mha = sb("mha", [P, G, F])
        mha_t = parts("mha_t", [P, KC, G, P])
        stats2 = sb("stats2", [P, G, 6])
        mv2 = sb("mv2", [P, 2, G, 2])
        vare2 = sb("vare2", [P, G])
        rstd2 = sb("rstd2", [P, G])
        out_s = sb("out_s", [P, 2, G, F])
        stage_w = wh[:].rearrange("p b n -> p (b n)")
        stage_wo = shared[:].rearrange("p (k n) -> p k n", k=K1)
        stage_s = qk_p[:].rearrange("p a b c d -> p (a b c d)")
        stage_s2 = qk_pt[:].rearrange("p a b c d -> p (a b c d)")
        a_r = gat_g[:].rearrange("p b n -> p (b n)")
        prod = gat_e[:].rearrange("p b n -> p (b n)")
        a2_r = x1b[:].rearrange("p a b c -> p (a b c)")
        pick_f = add_p[0:LOW + 2 * HA].rearrange("p h b m -> p (h b) m")
        adj_s = sb("adj_s", [P, P], I32)
        wa = sb("wa", [P, KC, 2 * HA])
        stage_f = sb("stage_f", [P, KC, P])

        small_w = [(w1, w1_w), (w2, w2_w), (WqT, wq_w), (WkT, wk_w), (WvT, wv_w), (WoT, wp_w)]

        def small_stage(i):
            s = stage_s if i < 4 else stage_s2
            i %= 4
            return s[:, i * KC * F:(i + 1) * KC * F].rearrange("p (k n) -> p k n", k=KC)

        bank = {"d0": ctx.enter_context(nc.psum_tensor("d0", [P, 1024], F32)),
                "d1": ctx.enter_context(nc.psum_tensor("d1", [P, 1024], F32))}
        for name in ("b4", "b5", "b6", "b7"):
            bank[name] = ctx.enter_context(nc.psum_tensor(name, [P, 512], F32))

        def at(product):
            return bank[PLACE[product]]

        by_name = {}

        def sems(names):
            new = {n: ctx.enter_context(nc.semaphore(n)) for n in names.split()}
            by_name.update(new)
            return new

        pe_done = sems("ffn1_done f_t_done qk_scores_done_0 qk_scores_done_1 ffn2_done add_scores_done_0 "
                    "add_scores_done_1 wh2_done_0 wh2_done_1 wh_done_0 wh_done_1 f2_t_done add2_scores_done "
                    "p2_t_done qk_probs_t_done_0 qk_probs_t_done_1 p_t_done_0 p_t_done_1 x1_t_done gat2_done "
                    "mha_done_0 mha_done_1 gat_done_0 gat_done_1 q_done k_done mha_t_done v_done proj_done")
        act_done = sems("x_t_high hid_ready f_t_high qk_exp_0 qk_exp_1 add_exp wh_ready_0 wh_ready_1 add2_exp "
                     "p2_t_ready qk_pt_ready_0 qk_pt_ready_1 p_t_ready_0 p_t_ready_1 x1_t_high gat2_exp gat2_high "
                     "slope_0 slope_1 slope2 gat_exp_0 gat_exp_1 q_ready k_ready mha_t_high")
        dve_done = sems("x_t_low hid_high hid_low f_t_low qk_max_0 qk_max_1 qk_sub_0 qk_sub_1 y_ready y_stats y_mv "
                     "leaky_0 leaky_1 add_max_ready add_sub y_scaled y_added y1_stats y1_mv wh2_ready_0 wh2_ready_1 "
                     "f2_high f2_low add_sum_ready add_rec_ready add_norm x1_ready f2_t_ready leaky2 "
                     "add2_max_ready add2_sub add2_sum_ready add2_rec_ready add2_norm x1_t_low gat2_ready "
                     "gat2_low mha_rec_0 mha_rec_1 mha_ready_0 mha_ready_1 gat_ready_0 gat_ready_1 gat_high_0 "
                     "gat_high_1 mha_t_low v_ready y2_ready y2_stats y2_mv out_ready")
        pool_done = sems("xb_ready vare_ready rstd_ready vare1_ready rstd1_ready vare2_ready rstd2_ready x1b_ready "
                      "gat_low_0 gat_low_1")
        x_landed = [ctx.enter_context(nc.semaphore(f"x_landed_{i}")) for i in range(2)]
        xres_landed = [ctx.enter_context(nc.semaphore(f"xres_landed_{i}")) for i in range(2)]
        stored = [ctx.enter_context(nc.semaphore(f"stored_{i}")) for i in range(2)]
        big_landed = ctx.enter_context(nc.semaphore("big_landed"))
        small_landed = ctx.enter_context(nc.semaphore("small_landed"))
        set_dve = ctx.enter_context(nc.semaphore("set_dve"))
        set_pe = ctx.enter_context(nc.semaphore("set_pe"))
        set_pool = ctx.enter_context(nc.semaphore("set_pool"))
        score_vectors = ctx.enter_context(nc.semaphore("score_vectors"))
        parts_high = ctx.enter_context(nc.semaphore("parts_high"))
        weights_ready = ctx.enter_context(nc.semaphore("weights_ready"))

        def flat(t, names):
            return t.rearrange(f"p {names} -> p ({names})")

        block = ctx.enter_context(nc.Block())

        def iterations(eng, body):
            def one(it):
                g = {s: it.plus(-lag) for s, lag in LAGS.items()}
                live = {s for s, c in g.items() if it.turn is not None or 0 <= c.base < NG}
                body(g, live, it)

            for i in range(FULL):
                one(Count(i))
            with eng.Fori(0, TURNS) as turn:
                for u in range(2):
                    one(Count(FULL + u, 2, turn))
            for i in range(NG, NG + LAGS["E"]):
                one(Count(i))

        @block.sync
        def _(sp):
            sp.dma_start(stage_w.rearrange("p (k h o) -> p k h o", k=KC, h=HA)[:, 0],
                         W_heads.rearrange("h (k p) o -> k p h o", k=KC)[0]).then_inc(big_landed, 16)
            sp.dma_start(stage_w.rearrange("p (k h o) -> p k h o", k=KC, h=HA)[:, 1],
                         W_heads.rearrange("h (k p) o -> k p h o", k=KC)[1]).then_inc(big_landed, 16)
            sp.dma_start(a_r, a_heads.rearrange("h o -> (h o)").rearrange("(a o) -> a o", a=1)
                         .broadcast_to([P, 2 * O1])).then_inc(big_landed, 16)
            sp.dma_start(stage_wo[:, :, 0:F], W_out.rearrange("(k p) n -> p k n", p=P)).then_inc(big_landed, 16)
            sp.dma_start(a2_r[:, 0:2 * F], a_out.rearrange("(a o) -> a o", a=1)
                         .broadcast_to([P, 2 * F])).then_inc(big_landed, 16)
            for i, (w, _) in enumerate(small_w):
                sp.dma_start(small_stage(i), w.rearrange("(k p) n -> p k n", p=P)).then_inc(small_landed, 16)

            def body(g, live, it):
                if "X" in live:
                    par = g["X"].base % 2
                    if g["X"].base >= 2:
                        sp.wait_ge(dve_done["x_t_low"], g["X"].plus(-1).value())
                    sp.dma_start(x_in[:, par], xT[:, g["X"].value()]).then_inc(x_landed[par], 16)
                if "B" in live:
                    par = g["B"].base % 2
                    if g["B"].base >= 2:
                        sp.wait_ge(pool_done["xb_ready"], g["B"].plus(-1).value())
                    sp.dma_start(x_res[:, par], x_groups[:, g["B"].value()]).then_inc(xres_landed[par], 16)
                if "E" in live:
                    par = g["E"].base % 2
                    sp.wait_ge(dve_done["out_ready"], g["E"].plus(1).value())
                    sp.dma_start(out_groups[:, g["E"].value()], out_s[:, par]).then_inc(stored[par], 16)

            iterations(sp, body)
            for par in range(2):
                sp.wait_ge(stored[par], 16 * (NG // 2))

        @block.tensor
        def _(pe):
            def read(product, it):
                ring = [p for p in PRODUCTS if p[1] == PLACE[product]]
                here = [p[0] for p in ring].index(product)
                for back in range(1, 8 * len(ring)):
                    _, _, stage, last_read = ring[(here - back) % len(ring)]
                    before = it.plus((here - back) // len(ring) - LAGS[stage])
                    if it.turn is not None or 0 <= before.base < NG:
                        return by_name[last_read], before.plus(1).value()
                return weights_ready, 2

            pe.wait_ge(big_landed, 16 * 5)
            pe.wait_ge(set_pool, 5)
            pe.wait_ge(set_dve, 2 * K1)
            for k in range(K1):
                mm = pe.matmul(bank["b4"][:, 0:F + 2], ones[:], stage_wo[:, k, :], start=(k == 0), stop=(k == K1 - 1))
            mm.then_inc(set_pe, 1)
            pe.wait_ge(small_landed, 16 * (len(small_w) + 12))
            for fc in range(KC):
                for oc in range(KC):
                    mm = pe.matmul(bank["b5"][:, fc:fc + 1], small_stage(0)[:, oc, fc * P:(fc + 1) * P],
                                   ones[:, 0:1], start=(oc == 0), stop=(oc == KC - 1))
            mm.then_inc(set_pe, 1)
            pe.wait_ge(weights_ready, 2)

            def split_product(dst, lhs, rhs):
                n = len(lhs[0])
                for k in range(n):
                    for i, (a, b) in enumerate(((0, 0), (0, 1), (1, 0))):
                        mm = pe.matmul(dst, lhs[a][k], rhs[b][k], start=(k == 0 and i == 0),
                                       stop=(k == n - 1 and i == 2))
                return mm

            def chunks(pair, index):
                return [[index(t, k) for k in range(KC)] for t in pair]

            def body(g, live, it):
                X, A, B, D, C = [stage in live for stage in "XABDC"]
                n_x, n_a, n_b, n_d, n_c = [g[stage].plus(1).value() for stage in "XABDC"]
                if A:
                    pe.wait_ge(dve_done["f_t_low"], n_a)
                    for hp in range(HA // 2):
                        pe.wait_ge(*read(f"add_scores_{hp}", it))
                        ps = at(f"add_scores_{hp}")
                        by_graph = ps[:].rearrange("p (h b m) -> p b h m", h=2, b=G)
                        pe.matmul(ps[:], ident_b[:], mask4[:].rearrange("p a n -> p (a n)"), start=True, stop=True)
                        for b in range(G):
                            pe.matmul(by_graph[:, b], f_t[:, b, :], pick_r[:, 2 * hp:2 * hp + 2, :],
                                      start=False, stop=False, skip_group_check=True)
                        for h in range(2):
                            mm = pe.matmul(ps[:, h * G * P:(h + 1) * G * P], pick_r[:, HA + 2 * hp + h, :],
                                           f_t[:].rearrange("p b n -> p (b n)"), start=False, stop=True,
                                           skip_group_check=True)
                        mm.then_inc(pe_done[f"add_scores_done_{hp}"], 1)
                if C:
                    pe.wait_ge(act_done["q_ready"], n_c)
                    pe.wait_ge(act_done["k_ready"], n_c)
                    pe.wait_ge(*read("qk_scores_0", it))
                    pe.wait_ge(*read("qk_scores_1", it))
                    halves = [at("qk_scores_0"), at("qk_scores_1")]
                    tiles = [halves[r // 2][:, (r % 2) * 512:(r % 2 + 1) * 512] for r in range(RT)]
                    for r in range(RT):
                        pe.matmul(tiles[r], ident_b[:], mask4[:].rearrange("p a n -> p (a n)"), start=True, stop=True)
                    for ob in range(OB):
                        for b in range(G):
                            j = ob * G + b
                            for r in range(RT):
                                rows = slice(r * DH, (r + 1) * DH)
                                mm = pe.matmul(tiles[r][:, j * P:(j + 1) * P], q_s[rows, ob, b, :], k_s[rows, ob, b, :],
                                               start=False, stop=True, skip_group_check=True)
                                if j == OB * G - 1 and r == 1:
                                    mm.then_inc(pe_done["qk_scores_done_0"], 1)
                    mm.then_inc(pe_done["qk_scores_done_1"], 1)
                if D:
                    pe.wait_ge(*read("ffn1", it))
                    ps = at("ffn1")
                    pe.wait_ge(act_done["gat2_high"], n_d)
                    pe.wait_ge(dve_done["gat2_low"], n_d)
                    for fc in range(KC):
                        mm = split_product(ps[:, fc * F:(fc + 1) * F],
                                           chunks(w1_w, lambda t, k: t[:, k, fc * P:(fc + 1) * P]),
                                           chunks(gat2_gp, lambda t, k: t[:, k].rearrange("p b n -> p (b n)")))
                    mm.then_inc(pe_done["ffn1_done"], 1)
                def wh2_product(b):
                    pe.wait_ge(*read(f"wh2_{b}", it))
                    ps = at(f"wh2_{b}")
                    pe.wait_ge(dve_done[f"gat_high_{b}"], n_b)
                    pe.wait_ge(pool_done[f"gat_low_{b}"], n_b)
                    mm = split_product(ps[:, 0:F + 2], [[t[:, b, k, :] for k in range(K1)] for t in gat_gp],
                                       [[t[:, k, :] for k in range(K1)] for t in wo_w])
                    mm.then_inc(pe_done[f"wh2_done_{b}"], 1)

                if B:
                    wh2_product(0)
                if D:
                    pe.wait_ge(*read("ffn2", it))
                    ps = at("ffn2")
                    pe.wait_ge(dve_done["hid_low"], n_d)
                    for b in range(G):
                        split_product(ps[:, b * F:(b + 1) * F], chunks(hid_p, lambda t, k: t[:, k, b, :]),
                                      chunks(w2_w, lambda t, k: t[:, k, :]))
                        for oc in range(KC):
                            for part in gat2_gp:
                                mm = pe.matmul(ps[:, b * F + oc * P:b * F + (oc + 1) * P], part[:, oc, b, :], ident_r[:],
                                               start=False, stop=(part is gat2_gp[1]),
                                               skip_group_check=True)
                    mm.then_inc(pe_done["ffn2_done"], 1)
                if B:
                    wh2_product(1)
                def wh_product(b):
                    pe.wait_ge(*read(f"wh_{b}", it))
                    ps = at(f"wh_{b}")
                    for half in range(2):
                        cols = slice(half * 512, (half + 1) * 512)
                        mm = split_product(ps[:, cols], chunks(x_t, lambda t, k: t[:, k, b, :]),
                                           chunks(wh_w, lambda t, k: t[:, k, cols]))
                    mm.then_inc(pe_done[f"wh_done_{b}"], 1)

                if A:
                    wh_product(0)
                if A:
                    wh_product(1)
                if A:
                    pe.wait_ge(dve_done["add_norm"], n_a)
                    for hp in range(HA // 2):
                        pe.wait_ge(*read(f"p_t_{hp}", it))
                        ps = at(f"p_t_{hp}")
                        for h in range(2):
                            for b in range(G):
                                c = (h * G + b) * P
                                mm = pe.transpose(ps[:, c:c + P], add_p[:, 2 * hp + h, b, :], ident[:])
                        mm.then_inc(pe_done[f"p_t_done_{hp}"], 1)
                if C:
                    for half in range(2):
                        pe.wait_ge(*read(f"qk_probs_t_{half}", it))
                        ps = at(f"qk_probs_t_{half}")
                        pe.wait_ge(act_done[f"qk_exp_{half}"], n_c)
                        for r in range(2):
                            for j in range(OB * G):
                                c = (r * OB * G + j) * P
                                mm = pe.transpose(ps[:, c:c + P], qk_p[:, 2 * half + r, j // G, j % G, :], ident[:])
                        mm.then_inc(pe_done[f"qk_probs_t_done_{half}"], 1)
                if B:
                    pe.wait_ge(*read("f2_t", it))
                    ps = at("f2_t")
                    pe.wait_ge(dve_done["f2_low"], n_b)
                    for b in range(G):
                        mm = pe.transpose(ps[0:4, b * P:(b + 1) * P], f2[:, b, :], ident[:])
                    mm.then_inc(pe_done["f2_t_done"], 1)
                if D:
                    pe.wait_ge(*read("x1_t", it))
                    ps = at("x1_t")
                    pe.wait_ge(dve_done["x1_ready"], n_d)
                    for kc in range(KC):
                        for b in range(G):
                            c = (kc * G + b) * P
                            mm = pe.transpose(ps[:, c:c + P], x1[:, b, kc * P:(kc + 1) * P], ident[:])
                    mm.then_inc(pe_done["x1_t_done"], 1)
                def gat_product(b):
                    pe.wait_ge(act_done["wh_ready_1"], n_a)
                    pe.wait_ge(act_done["p_t_ready_1"], n_a)
                    pe.wait_ge(*read(f"gat_{b}", it))
                    ps = at(f"gat_{b}")
                    for k in range(K1):
                        mm = pe.matmul(ps[:, k * P:(k + 1) * P], wh[:, b, k * P:(k + 1) * P],
                                       add_pt[:, k // KC, b, :], start=True, stop=True)
                    mm.then_inc(pe_done[f"gat_done_{b}"], 1)

                if A:
                    gat_product(0)
                if B:
                    pe.wait_ge(*read("add2_scores", it))
                    ps = at("add2_scores")
                    pe.wait_ge(dve_done["f2_t_ready"], n_b)
                    pe.matmul(ps[:, 0:G * P], ident_b[:], mask4[:, 0:G, :].rearrange("p a n -> p (a n)"),
                              start=True, stop=True)
                    for b in range(G):
                        pe.matmul(ps[:, b * P:(b + 1) * P], f2_t[:, b, :], pick2_r[:, 0, :], start=False, stop=False,
                                  skip_group_check=True)
                    pe.matmul(ps[:, 0:G * P], pick2_r[:, 1, :], f2_t[:].rearrange("p b n -> p (b n)"),
                              start=False, stop=True, skip_group_check=True).then_inc(pe_done["add2_scores_done"], 1)
                def mha_product(b):
                    pe.wait_ge(act_done["qk_pt_ready_1"], n_c)
                    pe.wait_ge(dve_done["v_ready"], n_c)
                    pe.wait_ge(*read(f"mha_{b}", it))
                    ps = at(f"mha_{b}")
                    for h in range(HM):
                        mm = pe.matmul(ps[:, h * (DH + 1):(h + 1) * (DH + 1)], qk_pt[:, h % RT, h // RT, b, :],
                                       v_s[:, b, h, :], start=True, stop=True)
                    mm.then_inc(pe_done[f"mha_done_{b}"], 1)

                if C:
                    mha_product(0)
                def qk_product(name, w):
                    pe.wait_ge(act_done["x1_t_high"], n_d)
                    pe.wait_ge(dve_done["x1_t_low"], n_d)
                    pe.wait_ge(*read(name, it))
                    ps = at(name)
                    for ob in range(OB):
                        mm = split_product(ps[:, ob * F:(ob + 1) * F],
                                           chunks(w, lambda t, k: t[:, k, ob * P:(ob + 1) * P]),
                                           chunks(x1_t, lambda t, k: t[:, k].rearrange("p b n -> p (b n)")))
                    mm.then_inc(pe_done[f"{name}_done"], 1)

                if D:
                    qk_product("q", wq_w)
                if C:
                    mha_product(1)
                if X:
                    pe.wait_ge(*read("f_t", it))
                    ps = at("f_t")
                    pe.wait_ge(act_done["x_t_high"], n_x)
                    pe.wait_ge(dve_done["x_t_low"], n_x)
                    mm = split_product(ps[:, 0:G * P], chunks(wf_w, lambda t, k: t[:, k, :]),
                                       chunks(x_t, lambda t, k: t[:, k].rearrange("p b n -> p (b n)")))
                    mm.then_inc(pe_done["f_t_done"], 1)
                if A:
                    gat_product(1)
                if D:
                    qk_product("k", wk_w)
                if C:
                    pe.wait_ge(*read("mha_t", it))
                    ps = at("mha_t")
                    pe.wait_ge(dve_done["mha_ready_1"], n_c)
                    for kc in range(KC):
                        for b in range(G):
                            c = (kc * G + b) * P
                            mm = pe.transpose(ps[:, c:c + P], mha[:, b, kc * P:(kc + 1) * P], ident[:])
                    mm.then_inc(pe_done["mha_t_done"], 1)
                if B:
                    pe.wait_ge(*read("p2_t", it))
                    ps = at("p2_t")
                    pe.wait_ge(dve_done["add2_norm"], n_b)
                    for b in range(G):
                        mm = pe.transpose(ps[:, b * P:(b + 1) * P], add2_p[:, b, :], ident[:])
                    mm.then_inc(pe_done["p2_t_done"], 1)
                if D:
                    pe.wait_ge(*read("v", it))
                    ps = at("v")
                    for b in range(G):
                        mm = split_product(ps[:, b * F:(b + 1) * F], chunks(x1_t, lambda t, k: t[:, k, b, :]),
                                           chunks(wv_w, lambda t, k: t[:, k, :]))
                    mm.then_inc(pe_done["v_done"], 1)
                if B:
                    pe.wait_ge(*read("gat2", it))
                    ps = at("gat2")
                    pe.wait_ge(act_done["p2_t_ready"], n_b)
                    for oc in range(KC):
                        for b in range(G):
                            c = (oc * G + b) * P
                            mm = pe.matmul(ps[:, c:c + P], wh2[:, b, oc * P:(oc + 1) * P], add2_pt[:, b, :],
                                           start=True, stop=True)
                    mm.then_inc(pe_done["gat2_done"], 1)
                if C:
                    pe.wait_ge(*read("proj", it))
                    ps = at("proj")
                    pe.wait_ge(act_done["mha_t_high"], n_c)
                    pe.wait_ge(dve_done["mha_t_low"], n_c)
                    for b in range(G):
                        mm = split_product(ps[:, b * F:(b + 1) * F], chunks(mha_t, lambda t, k: t[:, k, b, :]),
                                           chunks(wp_w, lambda t, k: t[:, k, :]))
                    mm.then_inc(pe_done["proj_done"], 1)

            iterations(pe, body)

        @block.scalar
        def _(act):
            for dst, src in ((gamma_r, ln_gamma), (beta_r, ln_beta), (b2_r, b2), (bv_r, bv), (bo_r, bo)):
                act.dma_start(dst[:], src.rearrange("(a o) -> a o", a=1).broadcast_to([P, F])).then_inc(small_landed, 16)
            for dst, src in ((b1_c, b1), (bq_c, bq), (bk_c, bk)):
                act.dma_start(dst[:], src).then_inc(small_landed, 16)
            act.dma_start(ident[:], eye).then_inc(small_landed, 16)
            act.dma_start(pick_f, pick).then_inc(small_landed, 16)
            act.dma_start(pick2_f[:], pick2).then_inc(small_landed, 16)
            act.dma_start(adj_s[:], adj).then_inc(small_landed, 16)
            act.wait_ge(big_landed, 16 * 5)
            act.activation(flat(wh_w[0][:], "k n"), stage_w, ACT.Copy).then_inc(parts_high, 1)
            act.wait_ge(set_dve, 2 * K1)
            act.activation(wo_w[0][:], stage_wo, ACT.Copy).then_inc(parts_high, 1)
            act.wait_ge(small_landed, 16 * (len(small_w) + 12))
            for i, (_, pair) in enumerate(small_w):
                act.activation(pair[0][:], small_stage(i), ACT.Copy).then_inc(parts_high, 1)
            act.wait_ge(score_vectors, 1)
            act.activation(wf_w[0][:], stage_f[:], ACT.Copy).then_inc(parts_high, 1)
            act.wait_ge(weights_ready, 2)

            def body(g, live, it):
                X, A, B, D, C = [stage in live for stage in "XABDC"]
                n_x, n_a, n_b, n_d, n_c = [g[stage].plus(1).value() for stage in "XABDC"]
                if A:
                    for hp in range(HA // 2):
                        act.wait_ge(pe_done[f"add_scores_done_{hp}"], n_a)
                        act.activation(flat(add_p[:, 2 * hp:2 * hp + 2], "h b m"), at(f"add_scores_{hp}")[:], ACT.Copy,
                                       scale=SLOPE).then_inc(act_done[f"slope_{hp}"], 1)
                if D:
                    act.wait_ge(pe_done["ffn1_done"], n_d)
                    for fc in range(KC):
                        a = act.activation(hid[:, fc].rearrange("p b n -> p (b n)"), at("ffn1")[:, fc * F:(fc + 1) * F],
                                           ACT.Relu, bias=b1_c[:, fc:fc + 1])
                    a.then_inc(act_done["hid_ready"], 1)
                if A:
                    act.wait_ge(dve_done["add_sub"], n_a)
                    t = add_p[:].rearrange("p h b m -> p (h b m)")
                    act.activation(t, t, ACT.Exp).then_inc(act_done["add_exp"], 1)
                if C:
                    for half in range(2):
                        act.wait_ge(dve_done[f"qk_sub_{half}"], n_c)
                        t = qk_p[:, 2 * half:2 * half + 2].rearrange("p r o b m -> p (r o b m)")
                        act.activation(t, t, ACT.Exp, scale=float(DH) ** -0.5).then_inc(act_done[f"qk_exp_{half}"], 1)
                def wh_copy(b):
                    act.wait_ge(pe_done[f"wh_done_{b}"], n_a)
                    a = act.activation(wh[:, b, :], at(f"wh_{b}")[:], ACT.Copy, bias=1.0)
                    a.then_inc(act_done[f"wh_ready_{b}"], 1)

                if A:
                    wh_copy(0)
                    wh_copy(1)
                if A:
                    for hp in range(2):
                        act.wait_ge(pe_done[f"p_t_done_{hp}"], n_a)
                        act.activation(add_pt[:, 2 * hp:2 * hp + 2].rearrange("p h b m -> p (h b m)"),
                                       at(f"p_t_{hp}")[:], ACT.Copy)\
                            .then_inc(act_done[f"p_t_ready_{hp}"], 1)
                if C:
                    for half in range(2):
                        act.wait_ge(pe_done[f"qk_probs_t_done_{half}"], n_c)
                        act.activation(qk_pt[:, 2 * half:2 * half + 2].rearrange("p r o b m -> p (r o b m)"),
                                       at(f"qk_probs_t_{half}")[:], ACT.Copy)\
                            .then_inc(act_done[f"qk_pt_ready_{half}"], 1)
                if D:
                    act.wait_ge(pe_done["x1_t_done"], n_d)
                    act.activation(x1_t[0][:].rearrange("p k b n -> p (k b n)"), at("x1_t")[:], ACT.Copy)\
                        .then_inc(act_done["x1_t_high"], 1)
                if B:
                    act.wait_ge(pe_done["add2_scores_done"], n_b)
                    act.activation(flat(add2_p[:], "b m"), at("add2_scores")[:, 0:G * P], ACT.Copy, scale=SLOPE)\
                        .then_inc(act_done["slope2"], 1)
                if A:
                    act.wait_ge(pe_done["gat_done_0"], n_a)
                    act.activation(gat_e[:, 0, :], at("gat_0")[:], ACT.Exp, bias=-1.0).then_inc(act_done["gat_exp_0"], 1)
                if B:
                    act.wait_ge(dve_done["add2_sub"], n_b)
                    t = add2_p[:].rearrange("p b m -> p (b m)")
                    act.activation(t, t, ACT.Exp).then_inc(act_done["add2_exp"], 1)
                if X:
                    par = g["X"].base % 2
                    act.wait_ge(x_landed[par], g["X"].half().plus(1).times(16).value())
                    act.activation(x_t[0][:].rearrange("p k b n -> p (k b n)"), x_in[:, par], ACT.Copy)\
                        .then_inc(act_done["x_t_high"], 1)
                def add_bias(name, dst, bias):
                    act.wait_ge(pe_done[f"{name}_done"], n_d)
                    for ob in range(OB):
                        a = act.activation(dst[:, ob].rearrange("p b n -> p (b n)"), at(name)[:, ob * F:(ob + 1) * F],
                                           ACT.Identity, bias=bias[:, ob:ob + 1])
                    a.then_inc(act_done[f"{name}_ready"], 1)

                if D:
                    add_bias("q", q_s, bq_c)
                if X:
                    act.wait_ge(pe_done["f_t_done"], n_x)
                    act.activation(f_t[:].rearrange("p b n -> p (b n)"), at("f_t")[0:LOW + 2 * HA, 0:G * P], ACT.Copy)\
                        .then_inc(act_done["f_t_high"], 1)
                if A:
                    act.wait_ge(pe_done["gat_done_1"], n_a)
                    act.activation(gat_e[:, 1, :], at("gat_1")[:], ACT.Exp, bias=-1.0).then_inc(act_done["gat_exp_1"], 1)
                if D:
                    add_bias("k", k_s, bk_c)
                if C:
                    act.wait_ge(pe_done["mha_t_done"], n_c)
                    act.activation(mha_t[0][:].rearrange("p k b n -> p (k b n)"), at("mha_t")[:], ACT.Copy)\
                        .then_inc(act_done["mha_t_high"], 1)
                if B:
                    act.wait_ge(pe_done["p2_t_done"], n_b)
                    act.activation(add2_pt[:].rearrange("p b n -> p (b n)"), at("p2_t")[:, 0:G * P], ACT.Copy)\
                        .then_inc(act_done["p2_t_ready"], 1)
                if B:
                    act.wait_ge(pe_done["gat2_done"], n_b)
                    act.activation(gat2_e.rearrange("p k b n -> p (k b n)"), at("gat2")[:], ACT.Exp,
                                   bias=-1.0).then_inc(act_done["gat2_exp"], 1)
                if B:
                    act.wait_ge(dve_done["gat2_ready"], n_b)
                    act.activation(gat2_gp[0][:], gat2_g, ACT.Copy).then_inc(act_done["gat2_high"], 1)

            iterations(act, body)

        @block.gpsimd
        def _(pool):
            pool.memset(ones[:], 1.0).then_inc(set_pool, 1)
            pool.memset(power[:], -0.5).then_inc(set_pool, 1)
            pool.memset(eps[:], EPS).then_inc(set_pool, 1)
            pool.memset(v_s[:], 1.0).then_inc(set_pool, 1)
            pool.memset(stage_f[:], 0.0).then_inc(set_pool, 1)
            lows = [(wo_w, stage_wo)] + [(pair, small_stage(i)) for i, (_, pair) in enumerate(small_w)]
            for i, (pair, src) in enumerate(lows + [(wf_w, stage_f[:])]):
                pool.wait_ge(parts_high, i + 2)
                p = pool.tensor_tensor(pair[1][:], src, pair[0][:].bitcast(F32), ALU.subtract)
            p.then_inc(weights_ready, 1)
            pool.wait_ge(weights_ready, 2)

            def inverse_deviation(var, vare, var_ready, vare_ready, rstd, rstd_ready, n):
                pool.wait_ge(var_ready, n)
                pool.tensor_tensor(vare[:], var, eps[:], ALU.add).then_inc(vare_ready, 1)
                pool.wait_ge(vare_ready, n)
                pool.tensor_tensor(rstd[:], vare[:], power[:], ALU.pow).then_inc(rstd_ready, 1)

            def body(g, live, it):
                A, D, C, E = ("A" in live), ("D" in live), ("C" in live), ("E" in live)
                n_a, n_d, n_c, n_e = [g[stage].plus(1).value() for stage in "ADCE"]
                if E:
                    inverse_deviation(mv2[:, g["E"].base % 2, :, 1], vare2, dve_done["y2_mv"], pool_done["vare2_ready"],
                                      rstd2, pool_done["rstd2_ready"], n_e)
                if D:
                    par = g["D"].base % 2
                    pool.wait_ge(xres_landed[par], g["D"].half().plus(1).times(16).value())
                    for b in range(G):
                        p = pool.tensor_tensor(xb[:, b], x_res[:, par, b], beta_r[:], ALU.add)
                    p.then_inc(pool_done["xb_ready"], 1)
                    inverse_deviation(mv[:, :, 1], vare, dve_done["y_mv"], pool_done["vare_ready"], rstd, pool_done["rstd_ready"], n_d)
                    inverse_deviation(mv1[:, :, 1], vare1, dve_done["y1_mv"], pool_done["vare1_ready"], rstd1,
                                      pool_done["rstd1_ready"], n_d)
                    pool.wait_ge(dve_done["x1_ready"], n_d)
                    for b in range(G):
                        p = pool.tensor_tensor(x1b[:, par, b], x1[:, b], bo_r[:], ALU.add)
                    p.then_inc(pool_done["x1b_ready"], 1)
                if A:
                    for b in range(G):
                        pool.wait_ge(dve_done[f"gat_high_{b}"], n_a)
                        pool.tensor_tensor(gat_gp[1][:, b].rearrange("p k n -> p (k n)"), gat_g[:, b, :],
                                           gat_gp[0][:, b].rearrange("p k n -> p (k n)").bitcast(F32), ALU.subtract)\
                            .then_inc(pool_done[f"gat_low_{b}"], 1)

            iterations(pool, body)

        @block.vector
        def _(dve):
            done = [0]

            def then(ins):
                done[0] += 1
                ins.then_inc(set_dve, 1)
                dve.wait_ge(set_dve, done[0])

            dve.wait_ge(big_landed, 16 * 5)
            dve.wait_ge(set_pool, 5)
            def dot(dst, u, v):
                place = done[0] % 8
                if done[0] >= 8:
                    dve.wait_ge(set_dve, done[0] - 7)
                dve.tensor_tensor_reduce(prod[:, place * F:(place + 1) * F], u, v, 1.0, 0.0, ALU.mult, ALU.add, dst)\
                    .then_inc(set_dve, 1)
                done[0] += 1

            for k in range(K1):
                for part in range(2):
                    dot(stage_wo[:, k, F + part:F + part + 1], stage_wo[:, k, 0:F], a2_r[:, part * F:(part + 1) * F])
            for kc in range(KC):
                for h in range(HA):
                    w = stage_w[:, kc * O1 + h * F:kc * O1 + (h + 1) * F]
                    for part in range(2):
                        dot(wa[:, kc, part * HA + h:part * HA + h + 1], w,
                            a_r[:, (2 * h + part) * F:(2 * h + part + 1) * F])
            dve.wait_ge(set_dve, done[0])
            dve.tensor_copy(stage_f[:, :, 0:2 * HA], wa[:])
            dve.tensor_copy(stage_f[:, :, LOW:LOW + 2 * HA], wa[:]).then_inc(score_vectors, 1)
            dve.wait_ge(parts_high, 1)
            dve.tensor_tensor(flat(wh_w[1][:], "k n"), stage_w, flat(wh_w[0][:], "k n").bitcast(F32), ALU.subtract)
            dve.wait_ge(small_landed, 16 * (len(small_w) + 12))
            dve.tensor_copy(ident_r[:], ident[:])
            dve.tensor_copy(ident_b[:], ident[:])
            dve.tensor_copy(pick_r[:], pick_f)
            dve.tensor_copy(pick2_r[:], pick2_f[:])
            dve.tensor_scalar(mask4[:], adj_s[:].unsqueeze(1).broadcast_to([P, 4, P]), 0, MASKED, ALU.is_le, ALU.mult)
            dve.wait_ge(set_pe, 1)
            dve.tensor_scalar(colsum[:, 0:F], bank["b4"][:, 0:F], -1.0, None, ALU.add)
            dve.tensor_copy(colsum[:, F:F + 2], bank["b4"][:, F:F + 2])
            dve.wait_ge(set_pe, 2)
            then(dve.tensor_tensor(b1_c[:], b1_c[:], bank["b5"][:, 0:KC], ALU.subtract))
            dve.tensor_scalar(b2_r[:], b2_r[:], -1.0, None, ALU.add)
            dve.memset(add2_max[:], 0.0).then_inc(weights_ready, 1)

            def row_stats(src, stats, ready):
                for b in range(G):
                    d = dve.bn_stats(stats[:, b], src[:, b])
                d.then_inc(ready, 1)

            def mean_variance(mv, stats, ready):
                for b in range(G):
                    d = dve.bn_aggr(mv[:, b], stats[:, b])
                d.then_inc(ready, 1)

            def body(g, live, it):
                X, A, B, D, C, E = [stage in live for stage in "XABDCE"]
                n_x, n_a, n_b, n_d, n_c, n_e = [g[stage].plus(1).value() for stage in "XABDCE"]
                if E:
                    dve.wait_ge(dve_done["y2_stats"], n_e)
                if A:
                    for hp in range(HA // 2):
                        dve.wait_ge(act_done[f"slope_{hp}"], n_a)
                        p2 = flat(add_p[:, 2 * hp:2 * hp + 2], "h b m")
                        dve.tensor_tensor(p2, at(f"add_scores_{hp}")[:], p2, ALU.max)\
                            .then_inc(dve_done[f"leaky_{hp}"], 1)
                if E:
                    mean_variance(mv2[:, g["E"].base % 2], stats2, dve_done["y2_mv"])
                if A:
                    dve.wait_ge(dve_done["leaky_1"], n_a)
                    p3 = add_p[:].rearrange("p h b m -> p (h b) m")
                    dve.tensor_reduce(add_max[:], p3, AX, ALU.max).then_inc(dve_done["add_max_ready"], 1)
                if A:
                    p3 = add_p[:].rearrange("p h b m -> p (h b) m")
                    dve.wait_ge(dve_done["add_max_ready"], n_a)
                    dve.tensor_tensor(p3, p3, add_max[:].unsqueeze(2).broadcast_to([P, HA * G, P]), ALU.subtract)\
                        .then_inc(dve_done["add_sub"], 1)
                if E:
                    par = g["E"].base % 2
                    dve.wait_ge(pool_done["rstd2_ready"], n_e)
                    if g["E"].base >= 2:
                        dve.wait_ge(stored[par], g["E"].half().times(16).value())
                    for b in range(G):
                        d = dve.tensor_scalar(out_s[:, par, b], y2[:, par, b], mv2[:, par, b, 0:1], rstd2[:, b:b + 1],
                                              ALU.subtract, ALU.mult)
                    d.then_inc(dve_done["out_ready"], 1)
                if D:
                    dve.wait_ge(act_done["hid_ready"], n_d)
                    dve.tensor_copy(hid_p[0][:], hid[:]).then_inc(dve_done["hid_high"], 1)
                    dve.wait_ge(dve_done["hid_high"], n_d)
                    dve.tensor_tensor(flat(hid_p[1][:], "k b n"), flat(hid[:], "k b n"),
                                      flat(hid_p[0][:], "k b n").bitcast(F32), ALU.subtract).then_inc(dve_done["hid_low"], 1)
                def qk_less_max(half):
                    dve.wait_ge(pe_done[f"qk_scores_done_{half}"], n_c)
                    s3 = at(f"qk_scores_{half}")[:].rearrange("p (j m) -> p j m", m=P)
                    mx = flat(qk_max[:, 2 * half:2 * half + 2], "r j")
                    dve.tensor_reduce(mx, s3, AX, ALU.max).then_inc(dve_done[f"qk_max_{half}"], 1)
                    dve.wait_ge(dve_done[f"qk_max_{half}"], n_c)
                    dve.tensor_tensor(qk_p[:, 2 * half:2 * half + 2].rearrange("p r o b m -> p (r o b) m"), s3,
                                      mx.unsqueeze(2).broadcast_to([P, 2 * OB * G, P]), ALU.subtract)\
                        .then_inc(dve_done[f"qk_sub_{half}"], 1)

                if C:
                    qk_less_max(0)
                if A:
                    dve.wait_ge(act_done["add_exp"], n_a)
                    p3 = add_p[:].rearrange("p h b m -> p (h b) m")
                    dve.tensor_reduce(add_sum[:], p3, AX, ALU.add).then_inc(dve_done["add_sum_ready"], 1)
                if D:
                    dve.wait_ge(pe_done["ffn2_done"], n_d)
                    dve.tensor_tensor(y[:], at("ffn2")[:].rearrange("p (b n) -> p b n", b=G),
                                      b2_r[:].unsqueeze(1).broadcast_to([P, G, F]), ALU.add).then_inc(dve_done["y_ready"], 1)
                    dve.wait_ge(dve_done["y_ready"], n_d)
                    row_stats(y, stats, dve_done["y_stats"])
                    dve.wait_ge(dve_done["y_stats"], n_d)
                if A:
                    dve.wait_ge(dve_done["add_sum_ready"], n_a)
                    dve.reciprocal(add_rec[:], add_sum[:]).then_inc(dve_done["add_rec_ready"], 1)
                if D:
                    mean_variance(mv, stats, dve_done["y_mv"])
                if C:
                    qk_less_max(1)
                if A:
                    dve.wait_ge(dve_done["add_rec_ready"], n_a)
                    dve.tensor_tensor(p3, p3, add_rec[:].unsqueeze(2).broadcast_to([P, HA * G, P]), ALU.mult)\
                        .then_inc(dve_done["add_norm"], 1)
                if D:
                    dve.wait_ge(pool_done["rstd_ready"], n_d)
                    for b in range(G):
                        d = dve.scalar_tensor_tensor(out=y[:, b], in0=y[:, b], scalar=mv[:, b, 0:1], in1=gamma_r[:],
                                                     op0=ALU.subtract, op1=ALU.mult)
                    d.then_inc(dve_done["y_scaled"], 1)
                    dve.wait_ge(dve_done["y_scaled"], n_d)
                    for b in range(G):
                        d = dve.scalar_tensor_tensor(out=y[:, b], in0=y[:, b], scalar=rstd[:, b:b + 1], in1=xb[:, b],
                                                     op0=ALU.mult, op1=ALU.add)
                    d.then_inc(dve_done["y_added"], 1)
                    dve.wait_ge(dve_done["y_added"], n_d)
                    row_stats(y, stats1, dve_done["y1_stats"])
                    dve.wait_ge(dve_done["y1_stats"], n_d)
                def wh2_values(b):
                    dve.wait_ge(pe_done[f"wh2_done_{b}"], n_b)
                    dve.tensor_tensor(wh2[:, b], at(f"wh2_{b}")[:, 0:F + 2], colsum[:], ALU.subtract)\
                        .then_inc(dve_done[f"wh2_ready_{b}"], 1)

                if B:
                    wh2_values(0)
                if D:
                    mean_variance(mv1, stats1, dve_done["y1_mv"])
                if B:
                    wh2_values(1)
                    dve.wait_ge(dve_done["wh2_ready_1"], n_b)
                    dve.tensor_copy(f2[:, :, 0:2].bitcast(F32R), wh2[:, :, F:F + 2]).then_inc(dve_done["f2_high"], 1)
                    dve.wait_ge(dve_done["f2_high"], n_b)
                    dve.tensor_tensor(f2[:, :, 2:4], wh2[:, :, F:F + 2], f2[:, :, 0:2], ALU.subtract)\
                        .then_inc(dve_done["f2_low"], 1)
                if D:
                    dve.wait_ge(pool_done["rstd1_ready"], n_d)
                    for b in range(G):
                        d = dve.tensor_scalar(x1[:, b], y[:, b], mv1[:, b, 0:1], rstd1[:, b:b + 1],
                                              ALU.subtract, ALU.mult)
                    d.then_inc(dve_done["x1_ready"], 1)
                if B:
                    dve.wait_ge(pe_done["f2_t_done"], n_b)
                    dve.tensor_copy(flat(f2_t[:], "b n"), at("f2_t")[0:4, 0:G * P]).then_inc(dve_done["f2_t_ready"], 1)
                if D:
                    dve.wait_ge(act_done["x1_t_high"], n_d)
                    dve.tensor_tensor(flat(x1_t[1][:], "k b n"), at("x1_t")[:], flat(x1_t[0][:], "k b n").bitcast(F32),
                                      ALU.subtract).then_inc(dve_done["x1_t_low"], 1)
                if B:
                    dve.wait_ge(act_done["slope2"], n_b)
                    p2 = flat(add2_p[:], "b m")
                    dve.tensor_tensor(p2, at("add2_scores")[:, 0:G * P], p2, ALU.max).then_inc(dve_done["leaky2"], 1)
                    dve.wait_ge(dve_done["leaky2"], n_b)
                    dve.tensor_reduce(add2_max[:], add2_p[:], AX, ALU.max).then_inc(dve_done["add2_max_ready"], 1)
                    dve.wait_ge(dve_done["add2_max_ready"], n_b)
                    dve.tensor_tensor(add2_p[:], add2_p[:], add2_max[:].unsqueeze(2).broadcast_to([P, G, P]),
                                      ALU.subtract).then_inc(dve_done["add2_sub"], 1)
                def gat(b):
                    dve.wait_ge(act_done[f"gat_exp_{b}"], n_a)
                    dve.scalar_tensor_tensor(out=gat_g[:, b], in0=gat_e[:, b], scalar=1.0, in1=at(f"gat_{b}")[:],
                                             op0=ALU.min, op1=ALU.max).then_inc(dve_done[f"gat_ready_{b}"], 1)
                    dve.wait_ge(dve_done[f"gat_ready_{b}"], n_a)
                    dve.tensor_copy(flat(gat_gp[0][:, b], "k n"), gat_g[:, b])\
                        .then_inc(dve_done[f"gat_high_{b}"], 1)

                if A:
                    gat(0)
                if X:
                    dve.wait_ge(act_done["x_t_high"], n_x)
                    dve.tensor_tensor(flat(x_t[1][:], "k b n"), x_in[:, g["X"].base % 2], flat(x_t[0][:], "k b n").bitcast(F32),
                                      ALU.subtract).then_inc(dve_done["x_t_low"], 1)
                if B:
                    dve.wait_ge(act_done["add2_exp"], n_b)
                    dve.tensor_reduce(add2_sum[:], add2_p[:], AX, ALU.add).then_inc(dve_done["add2_sum_ready"], 1)
                    dve.wait_ge(dve_done["add2_sum_ready"], n_b)
                    dve.reciprocal(add2_rec[:], add2_sum[:]).then_inc(dve_done["add2_rec_ready"], 1)
                    dve.wait_ge(dve_done["add2_rec_ready"], n_b)
                    dve.tensor_tensor(add2_p[:], add2_p[:], add2_rec[:].unsqueeze(2).broadcast_to([P, G, P]),
                                      ALU.mult).then_inc(dve_done["add2_norm"], 1)
                if C:
                    for b in range(G):
                        dve.wait_ge(pe_done[f"mha_done_{b}"], n_c)
                        o3 = at(f"mha_{b}")[:, 0:HM * (DH + 1)].rearrange("p (h d) -> p h d", h=HM)
                        dve.reciprocal(mha_rec[:, b], o3[:, :, DH]).then_inc(dve_done[f"mha_rec_{b}"], 1)
                        dve.wait_ge(dve_done[f"mha_rec_{b}"], n_c)
                        dve.tensor_tensor(mha[:, b].rearrange("p (h d) -> p h d", h=HM), o3[:, :, 0:DH],
                                          mha_rec[:, b].unsqueeze(2).broadcast_to([P, HM, DH]), ALU.mult)\
                            .then_inc(dve_done[f"mha_ready_{b}"], 1)
                if X:
                    dve.wait_ge(act_done["f_t_high"], n_x)
                    low = flat(f_t[LOW:LOW + 2 * HA], "b n")
                    dve.tensor_tensor(low, at("f_t")[LOW:LOW + 2 * HA, 0:G * P], low.bitcast(F32), ALU.subtract)\
                        .then_inc(dve_done["f_t_low"], 1)
                if A:
                    gat(1)
                if C:
                    dve.wait_ge(act_done["mha_t_high"], n_c)
                    dve.tensor_tensor(flat(mha_t[1][:], "k b n"), at("mha_t")[:], flat(mha_t[0][:], "k b n").bitcast(F32),
                                      ALU.subtract).then_inc(dve_done["mha_t_low"], 1)
                if D:
                    dve.wait_ge(pe_done["v_done"], n_d)
                    dve.tensor_tensor(v_s[:, :, :, 0:DH], at("v")[:].rearrange("p (b h d) -> p b h d", b=G, h=HM),
                                      bv_r[:].rearrange("p (h d) -> p h d", h=HM).unsqueeze(1)
                                      .broadcast_to([P, G, HM, DH]), ALU.add).then_inc(dve_done["v_ready"], 1)
                if B:
                    dve.wait_ge(act_done["gat2_exp"], n_b)
                    dve.scalar_tensor_tensor(out=flat(gat2_g, "k b n"), in0=flat(gat2_e, "k b n"), scalar=1.0,
                                             in1=at("gat2")[:], op0=ALU.min, op1=ALU.max).then_inc(dve_done["gat2_ready"], 1)
                if B:
                    dve.wait_ge(act_done["gat2_high"], n_b)
                    dve.tensor_tensor(flat(gat2_gp[1][:], "k b n"), flat(gat2_g, "k b n"),
                                      flat(gat2_gp[0][:], "k b n").bitcast(F32), ALU.subtract).then_inc(dve_done["gat2_low"], 1)
                if C:
                    par = g["C"].base % 2
                    dve.wait_ge(pe_done["proj_done"], n_c)
                    dve.wait_ge(pool_done["x1b_ready"], n_c)
                    dve.tensor_tensor(y2[:, par], at("proj")[:].rearrange("p (b n) -> p b n", b=G), x1b[:, par],
                                      ALU.add).then_inc(dve_done["y2_ready"], 1)
                    dve.wait_ge(dve_done["y2_ready"], n_c)
                    row_stats(y2[:, par], stats2, dve_done["y2_stats"])

            iterations(dve, body)


def kernel(x, adj, L0_gnn_W_heads, L0_gnn_a_heads, L0_gnn_W_out, L0_gnn_a_out, L0_gnn_w1, L0_gnn_b1, L0_gnn_w2,
           L0_gnn_b2, L0_gnn_ln_gamma, L0_gnn_ln_beta, L1_gnn_Wq, L1_gnn_bq, L1_gnn_Wk, L1_gnn_bk, L1_gnn_Wv,
           L1_gnn_bv, L1_gnn_Wo, L1_gnn_bo):
    import numpy as np
    import concourse.bacc as bacc
    from concourse.bass_utils import run_bass_kernel_spmd

    pick = np.zeros((LOW + 2 * HA, 2 * HA, P), np.float32)
    for c in range(2 * HA):
        pick[[c, LOW + c], c] = 1.0
    pick2 = np.zeros((4, 2, P), np.float32)
    for c in range(2):
        pick2[[c, 2 + c], c] = 1.0

    def columns(v):
        return np.asarray(v).reshape(-1, P).T

    x_t = np.asarray(x).reshape(-1, G, P, KC, P).transpose(4, 0, 3, 1, 2).reshape(P, -1, KC * G * P)
    arrays = {
        "x": x, "xT": x_t, "adj": adj, "W_heads": L0_gnn_W_heads, "a_heads": L0_gnn_a_heads, "W_out": L0_gnn_W_out,
        "a_out": L0_gnn_a_out, "w1": L0_gnn_w1, "b1": columns(L0_gnn_b1), "w2": L0_gnn_w2, "b2": L0_gnn_b2,
        "ln_gamma": L0_gnn_ln_gamma, "ln_beta": L0_gnn_ln_beta,
        "WqT": np.asarray(L1_gnn_Wq).T, "bq": columns(L1_gnn_bq), "WkT": np.asarray(L1_gnn_Wk).T, "bk": columns(L1_gnn_bk),
        "WvT": np.asarray(L1_gnn_Wv).T, "bv": L1_gnn_bv, "WoT": np.asarray(L1_gnn_Wo).T, "bo": L1_gnn_bo,
        "eye": np.eye(P, dtype=np.float32), "pick": pick, "pick2": pick2,
    }
    nc = bacc.Bacc("TRN2", target_bir_lowering=False, num_devices=1)
    feeds, args = {}, {}
    for name, a in arrays.items():
        a = np.ascontiguousarray(a)
        feeds[f"in_{name}"] = a
        args[name] = nc.dram_tensor(f"in_{name}", a.shape, mybir.dt.from_np(a.dtype), kind="ExternalInput").ap()
    out = nc.dram_tensor("out_x", tuple(np.shape(x)), F32, kind="ExternalOutput").ap()
    build(nc, out=out, **args)
    return run_bass_kernel_spmd(nc, [feeds], core_ids=[0]).results[0]["out_x"]
```

```python
from contextlib import ExitStack

import concourse.bass as bass
from concourse import mybir

F32 = mybir.dt.float32
F32R = mybir.dt.float32r
BF16 = mybir.dt.bfloat16
I32 = mybir.dt.int32
ALU = mybir.AluOpType
ACT = mybir.ActivationFunctionType
AX = mybir.AxisListType.X

P = 128
F = 256
KC = F // P
G = 2
HA = 4
O1 = HA * F
K1 = O1 // P
HM = 8
DH = F // HM
RT = P // DH
OB = HM // RT
MASKED = -1e11
SLOPE = 0.01
EPS = 1e-5
LAGS = {"X": 0, "A": 1, "B": 2, "D": 3, "C": 4, "E": 5}
LOW = 32

PRODUCTS = [
    ("add_scores_0", "b5", "A", "leaky_0"), ("add_scores_1", "b6", "A", "leaky_1"),
    ("proj", "b7", "E", "y2_ready"), ("qk_scores_0", "d0", "C", "qk_sub_0"), ("qk_scores_1", "d1", "C", "qk_sub_1"),
    ("ffn1", "b4", "D", "hid_high"), ("wh2_0", "b5", "B", "wh2_ready_0"), ("h_t", "b7", "D", "h_t_ready"),
    ("ffn2", "b4", "D", "y_ready"), ("wh2_1", "b7", "B", "wh2_ready_1"), ("wh_0", "d0", "A", "wh_ready_0"),
    ("wh_1", "d1", "A", "wh_ready_1"), ("p_t_0", "b5", "A", "p_t_ready_0"), ("p_t_1", "b6", "A", "p_t_ready_1"),
    ("qk_probs_t_0", "d0", "C", "qk_pt_ready_0"), ("v", "b6", "C", "v_ready"),
    ("f2_t", "b4", "B", "f2_t_ready"), ("gat_0", "d1", "A", "gat_ready_0"),
    ("x1_t", "b7", "D", "x1_t_low"), ("add2_scores", "b4", "B", "leaky2"), ("qk_probs_t_1", "d0", "C", "qk_pt_ready_1"),
    ("f_t", "b5", "X", "f_t_low"), ("q", "b7", "D", "q_ready"), ("mha_t", "b6", "C", "mha_t_low"),
    ("gat_1", "d0", "A", "gat_ready_1"), ("p2_t", "b4", "B", "p2_t_ready"), ("k", "b5", "D", "k_ready"),
    ("gat2", "b4", "B", "gat2_ready"),
]
PLACE = {product: place for product, place, _, _ in PRODUCTS}


class Count:

    def __init__(self, base, step=0, turn=None):
        self.base, self.step, self.turn = base, step, turn

    def first(self, n):
        return self.turn is None and self.base == n

    def plus(self, n):
        return Count(self.base + n, self.step, self.turn)

    def times(self, n):
        return Count(self.base * n, self.step * n, self.turn)

    def half(self):
        return Count(self.base // 2, self.step // 2, self.turn)

    def value(self):
        return self.base if self.turn is None else self.turn * self.step + self.base


def build(nc, x, xT, adj, W_heads, W_headsT, a_heads, W_out, W_outT, a_out, w1, b1, w2, b2, ln_gamma, ln_beta,
          WqT, bq, WkT, bk, WvT, bv, WoT, bo, eye, pick, pick2, out):
    NB = x.shape[0]
    NG = NB // G
    FULL = LAGS["E"] + 3
    TURNS = (NG - FULL) // 2
    assert FULL + 2 * TURNS == NG and x.shape[1:] == (P, F)

    x_groups = x.rearrange("(g b) n c -> n g b c", b=G)
    out_groups = out.rearrange("(g b) n c -> n g b c", b=G)

    with ExitStack() as ctx:
        def sb(name, shape, dt=F32):
            return ctx.enter_context(nc.sbuf_tensor(name, shape, dt))

        def parts(name, shape):
            return [sb(name + "_high", shape, F32R), sb(name + "_low", shape, F32R)]

        wh_w = parts("wh_w", [P, KC, O1])
        wf_w = parts("wf_w", [P, KC, P])
        wo_w = parts("wo_w", [P, K1, F + 2])
        w1_w = parts("w1_w", [P, KC, F])
        w2_w = parts("w2_w", [P, KC, F])
        wq_w = parts("wq_w", [P, KC, F])
        wk_w = parts("wk_w", [P, KC, F])
        wv_w = parts("wv_w", [P, KC, F])
        wp_w = parts("wp_w", [P, KC, F])
        ident = sb("ident", [P, P])
        ident_b = sb("ident_b", [P, P], BF16)
        mask4 = sb("mask4", [P, 4, P], BF16)
        pick_r = sb("pick_r", [LOW + 2 * HA, 2 * HA, P], F32R)
        pick2_f = sb("pick2_f", [4, 2, P])
        pick2_r = sb("pick2_r", [4, 2, P], F32R)
        ones_r = sb("ones_r", [P, P], F32R)
        colsum = sb("colsum", [P, F + 2])
        gamma_r = sb("gamma_r", [P, F])
        beta_r = sb("beta_r", [P, F])
        b2_r = sb("b2_r", [P, F])
        bo_r = sb("bo_r", [P, F])
        b1_c = sb("b1_c", [P, KC])
        bq_c = sb("bq_c", [P, OB])
        bk_c = sb("bk_c", [P, OB])
        bv_c = sb("bv_c", [P, OB])
        eps = sb("eps", [P, G])
        power = sb("power", [P, G])

        x_in = sb("x_in", [P, 2, KC * G * P])
        x_t = parts("x_t", [P, KC, G, P])
        f_t = sb("f_t", [LOW + 2 * HA, G, P], F32R)
        add_p = sb("add_p", [P, HA, G, P])
        add_max = sb("add_max", [P, HA * G])
        add_sum = sb("add_sum", [P, HA * G])
        add_rec = sb("add_rec", [P, HA * G])
        add_pt = sb("add_pt", [P, HA, G, P])
        wh = sb("wh", [P, G, O1])
        gat_e = sb("gat_e", [P, G, O1])
        gat_g = sb("gat_g", [P, G, O1])
        gat_gp = parts("gat_gp", [P, G, K1, P])
        wh2 = sb("wh2", [P, G, F + 2])
        f2 = sb("f2", [P, G, 4])
        f2_t = sb("f2_t", [4, G, P], F32R)
        add2_p = sb("add2_p", [P, G, P])
        add2_max = sb("add2_max", [P, G])
        add2_sum = sb("add2_sum", [P, G])
        add2_rec = sb("add2_rec", [P, G])
        add2_pt = sb("add2_pt", [P, G, P])
        shared = sb("shared", [P, K1 * (F + 2)])
        gat2_e = shared[:, 0:512].rearrange("p (k b n) -> p k b n", k=KC, b=G)
        gat2_g = shared[:, 512:1024].rearrange("p (k b n) -> p k b n", k=KC, b=G)
        y2 = shared[:, 1024:2048].rearrange("p (a b n) -> p a b n", a=2, b=G)
        gat2_gp = parts("gat2_gp", [P, KC, G, P])
        h_res = sb("h_res", [P, G, F])
        hid = sb("hid", [P, KC, G, P])
        hid_p = parts("hid_p", [P, KC, G, P])
        y = sb("y", [P, G, F])
        stats = sb("stats", [P, G, 6])
        mv = sb("mv", [P, G, 2])
        vare = sb("vare", [P, G])
        rstd = sb("rstd", [P, G])
        x_res = sb("x_res", [P, 2, G, F])
        xb = sb("xb", [P, G, F])
        stats1 = sb("stats1", [P, G, 6])
        mv1 = sb("mv1", [P, G, 2])
        vare1 = sb("vare1", [P, G])
        rstd1 = sb("rstd1", [P, G])
        x1 = sb("x1", [P, G, F])
        x1b = sb("x1b", [P, 2, G, F])
        x1_t = parts("x1_t", [P, KC, G, P])
        q_s = sb("q_s", [P, OB, G, P])
        k_s = sb("k_s", [P, OB, G, P])
        v_s = sb("v_s", [P, G, HM, DH])
        qk_p = sb("qk_p", [P, RT, OB, G, P])
        qk_max = sb("qk_max", [P, RT, OB * G])
        qk_pt = sb("qk_pt", [P, RT, OB, G, P])
        qk_sum = sb("qk_sum", [P, RT, OB * G])
        qk_rec = sb("qk_rec", [P, RT, OB * G])
        mha_t = parts("mha_t", [P, KC, G, P])
        stats2 = sb("stats2", [P, G, 6])
        mv2 = sb("mv2", [P, 2, G, 2])
        vare2 = sb("vare2", [P, G])
        rstd2 = sb("rstd2", [P, G])
        zero = sb("zero", [P, G])
        minus_mean2 = sb("minus_mean2", [P, G])
        shift2 = sb("shift2", [P, G])
        out_s = sb("out_s", [P, 2, G, F])
        stage_w = wh[:].rearrange("p b n -> p (b n)")
        stage_wo = shared[:].rearrange("p (k n) -> p k n", k=K1)
        stage_s = qk_pt[:].rearrange("p a b c d -> p (a b c d)")
        stage_s2 = out_s[:].rearrange("p a b c -> p (a b c)")
        stage_wt = gat_g[:].rearrange("p b n -> p (b n)").rearrange("p (h oc c) -> p h oc c", h=HA, oc=KC)
        stage_wot = qk_p[:].rearrange("p a b c d -> p (a b c d)").rearrange("p (oc k) -> p oc k", oc=KC)
        ones = y[:, 0, 0:P]
        pick_f = add_p[0:LOW + 2 * HA].rearrange("p h b m -> p (h b) m")
        adj_s = sb("adj_s", [P, P], I32)
        a_cols = sb("a_cols", [P, HA, KC, 2])
        ao_cols = sb("ao_cols", [P, KC, 2])
        stage_f = sb("stage_f", [P, KC, P])

        small_w = [(w1, w1_w), (w2, w2_w), (WqT, wq_w), (WkT, wk_w), (WvT, wv_w), (WoT, wp_w)]

        small_all = 16 * (len(small_w) + 8)

        def small_stage(i):
            s = stage_s if i < 4 else stage_s2
            i %= 4
            return s[:, i * KC * F:(i + 1) * KC * F].rearrange("p (k n) -> p k n", k=KC)

        bank = {"d0": ctx.enter_context(nc.psum_tensor("d0", [P, 1024], F32)),
                "d1": ctx.enter_context(nc.psum_tensor("d1", [P, 1024], F32))}
        for name in ("b4", "b5", "b6", "b7"):
            bank[name] = ctx.enter_context(nc.psum_tensor(name, [P, 512], F32))

        def at(product):
            return bank[PLACE[product]]

        by_name = {}

        def sems(names):
            new = {n: ctx.enter_context(nc.semaphore(n)) for n in names.split()}
            by_name.update(new)
            return new

        pe_done = sems("h_t_done ffn1_done f_t_done qk_scores_done_0 qk_scores_done_1 ffn2_done "
                       "add_scores_done_0 add_scores_done_1 wh2_done_0 wh2_done_1 wh_done_0 wh_done_1 f2_t_done "
                       "add2_scores_done p2_t_done qk_probs_t_done_0 qk_probs_t_done_1 p_t_done_0 p_t_done_1 "
                       "x1_t_done gat2_done gat_done_0 gat_done_1 q_done k_done mha_t_done v_done proj_done")
        act_done = sems("x_t_high hid_ready hid_high f_t_high qk_exp_0 qk_exp_1 add_exp wh_ready_0 wh_ready_1 "
                        "add2_exp p2_t_ready qk_pt_ready_0 qk_pt_ready_1 p_t_ready_0 p_t_ready_1 x1_t_high "
                        "gat2_exp gat2_high slope_0 slope_1 slope2 gat_exp_0 gat_exp_1 q_ready k_ready "
                        "mha_t_high v_ready gat_high_0 out_ready h_t_ready")
        dve_done = sems("x_t_low hid_low f_t_low qk_max_0 qk_max_1 qk_sub_0 qk_sub_1 y_ready y_stats y_mv "
                        "leaky_0 leaky_1 add_max_ready add_sub y_scaled y_added y1_stats y1_mv wh2_ready_0 "
                        "wh2_ready_1 f2_high f2_low add_sum_ready add_rec_ready add_norm x1_ready f2_t_ready "
                        "leaky2 add2_max_ready add2_sub add2_sum_ready add2_rec_ready add2_norm x1_t_low "
                        "gat2_ready gat2_low qk_sum_ready_0 qk_sum_ready_1 qk_rec_ready_0 qk_rec_ready_1 "
                        "gat_ready_0 gat_ready_1 gat_high_1 mha_t_low y2_ready y2_stats y2_mv")
        pool_done = sems("xb_ready vare_ready rstd_ready vare1_ready rstd1_ready vare2_ready rstd2_ready "
                         "shift2_ready minus_mean2 x1b_ready h_ready gat_low_0 gat_low_1 qk_norm_0 qk_norm_1")
        gat_high = [act_done["gat_high_0"], dve_done["gat_high_1"]]
        x_landed = [ctx.enter_context(nc.semaphore(f"x_landed_{i}")) for i in range(2)]
        xres_landed = [ctx.enter_context(nc.semaphore(f"xres_landed_{i}")) for i in range(2)]
        stored = [ctx.enter_context(nc.semaphore(f"stored_{i}")) for i in range(2)]
        prepared = sems("heads_t_landed heads_landed masks_landed out_landed small_landed pool_constants "
                        "head_scores head_scores_copied wf_high wf_parts idents_ready mask_ready wh_high wh_low "
                        "out_scores out_scores_copied wo_high wo_parts sums_done b1_ready small_high small_low")

        def flat(t, names):
            return t.rearrange(f"p {names} -> p ({names})")

        block = ctx.enter_context(nc.Block())

        def iterations(eng, body):
            def one(it):
                g = {s: it.plus(-lag) for s, lag in LAGS.items()}
                live = {s for s, c in g.items() if it.turn is not None or 0 <= c.base < NG}
                body(g, live, it)

            for i in range(FULL):
                one(Count(i))
            with eng.Fori(0, TURNS) as turn:
                for u in range(2):
                    one(Count(FULL + u, 2, turn))
            for i in range(NG, NG + LAGS["E"]):
                one(Count(i))

        @block.sync
        def _(sp):
            sp.dma_start(stage_wt, W_headsT).then_inc(prepared["heads_t_landed"], 16)
            for kc in range(KC):
                sp.dma_start(stage_w.rearrange("p (k h o) -> p k h o", k=KC, h=HA)[:, kc],
                             W_heads.rearrange("h (k p) o -> k p h o", k=KC)[kc]).then_inc(prepared["heads_landed"], 16)

            def body(g, live, it):
                if it.first(1):
                    sp.dma_start(stage_wot, W_outT).then_inc(prepared["out_landed"], 16)
                    sp.dma_start(stage_wo[:, :, 0:F], W_out.rearrange("(k p) n -> p k n", p=P))\
                        .then_inc(prepared["out_landed"], 16)
                if it.first(2):
                    for i, (w, _) in enumerate(small_w):
                        sp.dma_start(small_stage(i), w.rearrange("(k p) n -> p k n", p=P))\
                            .then_inc(prepared["small_landed"], 16)
                    for dst, src in ((gamma_r, ln_gamma), (beta_r, ln_beta), (b2_r, b2), (bo_r, bo)):
                        sp.dma_start(dst[:], src.rearrange("(a o) -> a o", a=1).broadcast_to([P, F]))\
                            .then_inc(prepared["small_landed"], 16)
                    for dst, src in ((b1_c, b1), (bq_c, bq), (bk_c, bk), (bv_c, bv)):
                        sp.dma_start(dst[:], src).then_inc(prepared["small_landed"], 16)
                if "X" in live:
                    par = g["X"].base % 2
                    if g["X"].base >= 2:
                        sp.wait_ge(dve_done["x_t_low"], g["X"].plus(-1).value())
                    sp.dma_start(x_in[:, par], xT[:, g["X"].value()]).then_inc(x_landed[par], 16)
                if "B" in live:
                    par = g["B"].base % 2
                    if g["B"].base >= 2:
                        sp.wait_ge(pool_done["xb_ready"], g["B"].plus(-1).value())
                    sp.dma_start(x_res[:, par], x_groups[:, g["B"].value()]).then_inc(xres_landed[par], 16)
                if "E" in live:
                    par = g["E"].base % 2
                    sp.wait_ge(act_done["out_ready"], g["E"].plus(1).value())
                    sp.dma_start(out_groups[:, g["E"].value()], out_s[:, par]).then_inc(stored[par], 16)

            iterations(sp, body)
            for par in range(2):
                sp.wait_ge(stored[par], 16 * (NG // 2))

        @block.tensor
        def _(pe):
            def read(product, it):
                ring = [p for p in PRODUCTS if p[1] == PLACE[product]]
                here = [p[0] for p in ring].index(product)
                for back in range(1, 8 * len(ring)):
                    _, _, stage, last_read = ring[(here - back) % len(ring)]
                    before = it.plus((here - back) // len(ring) - LAGS[stage])
                    if it.turn is not None or 0 <= before.base < NG:
                        return by_name[last_read], before.plus(1).value()
                return prepared["wf_parts"], 1

            pe.wait_ge(prepared["heads_t_landed"], 16 * 2)
            for kc in range(KC):
                for h in range(HA):
                    c = (kc * HA + h) * 2
                    for oc in range(KC):
                        mm = pe.matmul(bank["b7"][:, c:c + 2], stage_wt[:, h, oc, kc * P:(kc + 1) * P], a_cols[:, h, oc],
                                       start=(oc == 0), stop=(oc == KC - 1))
            mm.then_inc(prepared["head_scores"], 1)

            def split_product(dst, lhs, rhs):
                n = len(lhs[0])
                for k in range(n):
                    for i, (a, b) in enumerate(((0, 0), (0, 1), (1, 0))):
                        mm = pe.matmul(dst, lhs[a][k], rhs[b][k], start=(k == 0 and i == 0),
                                       stop=(k == n - 1 and i == 2))
                return mm

            def chunks(pair, index):
                return [[index(t, k) for k in range(KC)] for t in pair]

            def body(g, live, it):
                X, A, B, D, C, E = [stage in live for stage in "XABDCE"]
                n_x, n_a, n_b, n_d, n_c, n_e = [g[stage].plus(1).value() for stage in "XABDCE"]
                if it.first(1):
                    pe.wait_ge(prepared["idents_ready"], 4)
                    pe.wait_ge(prepared["mask_ready"], 1)
                if it.first(2):
                    pe.wait_ge(prepared["wo_parts"], 1)
                    pe.wait_ge(dve_done["gat_ready_0"], 1)
                    for part in wo_w:
                        for k in range(K1):
                            mm = pe.matmul(bank["d1"][:, 0:F + 2], ones_r[:], part[:, k, :],
                                           start=(k == 0 and part is wo_w[0]),
                                           stop=(k == K1 - 1 and part is wo_w[1]))
                    mm.then_inc(prepared["sums_done"], 1)
                    pe.wait_ge(prepared["small_landed"], small_all)
                    for fc in range(KC):
                        for oc in range(KC):
                            mm = pe.matmul(bank["d1"][:, 512 + fc:513 + fc], small_stage(0)[:, oc, fc * P:(fc + 1) * P],
                                           ones[:, 0:1], start=(oc == 0), stop=(oc == KC - 1))
                    mm.then_inc(prepared["sums_done"], 1)
                if it.first(3):
                    pe.wait_ge(prepared["small_low"], len(small_w))
                if A:
                    pe.wait_ge(dve_done["f_t_low"], n_a)
                    for hp in range(HA // 2):
                        pe.wait_ge(*read(f"add_scores_{hp}", it))
                        ps = at(f"add_scores_{hp}")
                        by_graph = ps[:].rearrange("p (h b m) -> p b h m", h=2, b=G)
                        pe.matmul(ps[:], ident_b[:], mask4[:].rearrange("p a n -> p (a n)"), start=True, stop=True)
                        for b in range(G):
                            pe.matmul(by_graph[:, b], f_t[:, b, :], pick_r[:, 2 * hp:2 * hp + 2, :],
                                      start=False, stop=False, skip_group_check=True)
                        for h in range(2):
                            mm = pe.matmul(ps[:, h * G * P:(h + 1) * G * P], pick_r[:, HA + 2 * hp + h, :],
                                           f_t[:].rearrange("p b n -> p (b n)"), start=False, stop=True,
                                           skip_group_check=True)
                        mm.then_inc(pe_done[f"add_scores_done_{hp}"], 1)

                def qk_scores(ob):
                    halves = [at("qk_scores_0"), at("qk_scores_1")]
                    tiles = [halves[r // 2][:, (r % 2) * 512:(r % 2 + 1) * 512] for r in range(RT)]
                    for b in range(G):
                        j = ob * G + b
                        for r in range(RT):
                            rows = slice(r * DH, (r + 1) * DH)
                            mm = pe.matmul(tiles[r][:, j * P:(j + 1) * P], q_s[rows, ob, b, :], k_s[rows, ob, b, :],
                                           start=False, stop=True, skip_group_check=True)
                            if j == OB * G - 1 and r == 1:
                                mm.then_inc(pe_done["qk_scores_done_0"], 1)
                    return mm

                if C:
                    pe.wait_ge(act_done["q_ready"], n_c)
                    pe.wait_ge(act_done["k_ready"], n_c)
                    for half in range(2):
                        pe.wait_ge(*read(f"qk_scores_{half}", it))
                        for r in range(2):
                            pe.matmul(at(f"qk_scores_{half}")[:, r * 512:(r + 1) * 512], ident_b[:],
                                      mask4[:].rearrange("p a n -> p (a n)"), start=True, stop=True)
                    qk_scores(0)
                if E:
                    pe.wait_ge(*read("proj", it))
                    ps = at("proj")
                    pe.wait_ge(act_done["mha_t_high"], n_e)
                    pe.wait_ge(dve_done["mha_t_low"], n_e)
                    for b in range(G):
                        mm = split_product(ps[:, b * F:(b + 1) * F], chunks(mha_t, lambda t, k: t[:, k, b, :]),
                                           chunks(wp_w, lambda t, k: t[:, k, :]))
                    mm.then_inc(pe_done["proj_done"], 1)
                if C:
                    qk_scores(1).then_inc(pe_done["qk_scores_done_1"], 1)
                if D:
                    pe.wait_ge(*read("ffn1", it))
                    ps = at("ffn1")
                    pe.wait_ge(act_done["gat2_high"], n_d)
                    pe.wait_ge(dve_done["gat2_low"], n_d)
                    for fc in range(KC):
                        mm = split_product(ps[:, fc * F:(fc + 1) * F],
                                           chunks(w1_w, lambda t, k: t[:, k, fc * P:(fc + 1) * P]),
                                           chunks(gat2_gp, lambda t, k: t[:, k].rearrange("p b n -> p (b n)")))
                    mm.then_inc(pe_done["ffn1_done"], 1)
                def wh2_product(b):
                    pe.wait_ge(*read(f"wh2_{b}", it))
                    ps = at(f"wh2_{b}")
                    pe.wait_ge(gat_high[b], n_b)
                    pe.wait_ge(pool_done[f"gat_low_{b}"], n_b)
                    mm = split_product(ps[:, 0:F + 2], [[t[:, b, k, :] for k in range(K1)] for t in gat_gp],
                                       [[t[:, k, :] for k in range(K1)] for t in wo_w])
                    mm.then_inc(pe_done[f"wh2_done_{b}"], 1)

                if B:
                    wh2_product(0)
                if D:
                    pe.wait_ge(*read("h_t", it))
                    ps = at("h_t")
                    pe.wait_ge(dve_done["gat2_ready"], n_d)
                    for b in range(G):
                        for oc in range(KC):
                            c = b * F + oc * P
                            mm = pe.transpose(ps[:, c:c + P], gat2_g[:, oc, b, :], ident[:])
                    mm.then_inc(pe_done["h_t_done"], 1)
                    pe.wait_ge(*read("ffn2", it))
                    ps = at("ffn2")
                    pe.wait_ge(dve_done["hid_low"], n_d)
                    for b in range(G):
                        mm = split_product(ps[:, b * F:(b + 1) * F], chunks(hid_p, lambda t, k: t[:, k, b, :]),
                                           chunks(w2_w, lambda t, k: t[:, k, :]))
                    mm.then_inc(pe_done["ffn2_done"], 1)
                if B:
                    wh2_product(1)

                def wh_product(b):
                    pe.wait_ge(*read(f"wh_{b}", it))
                    ps = at(f"wh_{b}")
                    for half in range(2):
                        cols = slice(half * 512, (half + 1) * 512)
                        mm = split_product(ps[:, cols], chunks(x_t, lambda t, k: t[:, k, b, :]),
                                           chunks(wh_w, lambda t, k: t[:, k, cols]))
                    mm.then_inc(pe_done[f"wh_done_{b}"], 1)

                if it.first(1):
                    pe.wait_ge(prepared["wh_low"], 1)
                if it.first(2):
                    pe.wait_ge(prepared["b1_ready"], 1)
                if A:
                    wh_product(0)
                    pe.wait_ge(dve_done["add_norm"], n_a)
                    for hp in range(HA // 2):
                        pe.wait_ge(*read(f"p_t_{hp}", it))
                        ps = at(f"p_t_{hp}")
                        for h in range(2):
                            for b in range(G):
                                c = (h * G + b) * P
                                mm = pe.transpose(ps[:, c:c + P], add_p[:, 2 * hp + h, b, :], ident[:])
                        mm.then_inc(pe_done[f"p_t_done_{hp}"], 1)
                    wh_product(1)

                def qk_probs_transposed(half):
                    pe.wait_ge(*read(f"qk_probs_t_{half}", it))
                    ps = at(f"qk_probs_t_{half}")
                    pe.wait_ge(pool_done[f"qk_norm_{half}"], n_c)
                    for r in range(2):
                        for j in range(OB * G):
                            c = (r * OB * G + j) * P
                            mm = pe.transpose(ps[:, c:c + P], qk_p[:, 2 * half + r, j // G, j % G, :], ident[:])
                    mm.then_inc(pe_done[f"qk_probs_t_done_{half}"], 1)

                if C:
                    qk_probs_transposed(0)
                    pe.wait_ge(*read("v", it))
                    ps = at("v")
                    for b in range(G):
                        mm = split_product(ps[:, b * F:(b + 1) * F], chunks(x1_t, lambda t, k: t[:, k, b, :]),
                                           chunks(wv_w, lambda t, k: t[:, k, :]))
                    mm.then_inc(pe_done["v_done"], 1)
                if B:
                    pe.wait_ge(*read("f2_t", it))
                    ps = at("f2_t")
                    pe.wait_ge(dve_done["f2_low"], n_b)
                    for b in range(G):
                        mm = pe.transpose(ps[0:4, b * P:(b + 1) * P], f2[:, b, :], ident[:])
                    mm.then_inc(pe_done["f2_t_done"], 1)

                def gat_product(b):
                    pe.wait_ge(act_done[f"wh_ready_{b}"], n_a)
                    pe.wait_ge(act_done["p_t_ready_1"], n_a)
                    pe.wait_ge(*read(f"gat_{b}", it))
                    ps = at(f"gat_{b}")
                    for k in range(K1):
                        mm = pe.matmul(ps[:, k * P:(k + 1) * P], wh[:, b, k * P:(k + 1) * P],
                                       add_pt[:, k // KC, b, :], start=True, stop=True)
                    mm.then_inc(pe_done[f"gat_done_{b}"], 1)

                if A:
                    gat_product(0)
                if it.first(1):
                    pe.wait_ge(prepared["out_landed"], 16 * 3)
                    for k in range(K1):
                        for oc in range(KC):
                            mm = pe.matmul(bank["b6"][:, 2 * k:2 * k + 2], stage_wot[:, oc, k * P:(k + 1) * P],
                                           ao_cols[:, oc], start=(oc == 0), stop=(oc == KC - 1))
                    mm.then_inc(prepared["out_scores"], 1)
                if D:
                    pe.wait_ge(*read("x1_t", it))
                    ps = at("x1_t")
                    pe.wait_ge(dve_done["x1_ready"], n_d)
                    for kc in range(KC):
                        for b in range(G):
                            c = (kc * G + b) * P
                            mm = pe.transpose(ps[:, c:c + P], x1[:, b, kc * P:(kc + 1) * P], ident[:])
                    mm.then_inc(pe_done["x1_t_done"], 1)
                if B:
                    pe.wait_ge(*read("add2_scores", it))
                    ps = at("add2_scores")
                    pe.wait_ge(dve_done["f2_t_ready"], n_b)
                    pe.matmul(ps[:, 0:G * P], ident_b[:], mask4[:, 0:G, :].rearrange("p a n -> p (a n)"),
                              start=True, stop=True)
                    for b in range(G):
                        pe.matmul(ps[:, b * P:(b + 1) * P], f2_t[:, b, :], pick2_r[:, 0, :], start=False, stop=False,
                                  skip_group_check=True)
                    pe.matmul(ps[:, 0:G * P], pick2_r[:, 1, :], f2_t[:].rearrange("p b n -> p (b n)"),
                              start=False, stop=True, skip_group_check=True).then_inc(pe_done["add2_scores_done"], 1)
                if C:
                    qk_probs_transposed(1)
                if X:
                    pe.wait_ge(*read("f_t", it))
                    ps = at("f_t")
                    pe.wait_ge(act_done["x_t_high"], n_x)
                    pe.wait_ge(dve_done["x_t_low"], n_x)
                    mm = split_product(ps[:, 0:G * P], chunks(wf_w, lambda t, k: t[:, k, :]),
                                       chunks(x_t, lambda t, k: t[:, k].rearrange("p b n -> p (b n)")))
                    mm.then_inc(pe_done["f_t_done"], 1)

                def qk_product(name, w):
                    pe.wait_ge(act_done["x1_t_high"], n_d)
                    pe.wait_ge(dve_done["x1_t_low"], n_d)
                    pe.wait_ge(*read(name, it))
                    ps = at(name)
                    for ob in range(OB):
                        mm = split_product(ps[:, ob * F:(ob + 1) * F],
                                           chunks(w, lambda t, k: t[:, k, ob * P:(ob + 1) * P]),
                                           chunks(x1_t, lambda t, k: t[:, k].rearrange("p b n -> p (b n)")))
                    mm.then_inc(pe_done[f"{name}_done"], 1)

                if D:
                    qk_product("q", wq_w)
                if C:
                    pe.wait_ge(*read("mha_t", it))
                    ps = at("mha_t")
                    pe.wait_ge(act_done["qk_pt_ready_1"], n_c)
                    pe.wait_ge(act_done["v_ready"], n_c)
                    for ob in range(OB):
                        for b in range(G):
                            c = (ob * G + b) * P
                            for r in range(RT):
                                mm = pe.matmul(ps[r * DH:(r + 1) * DH, c:c + P], v_s[:, b, ob * RT + r, :],
                                               qk_pt[:, r, ob, b, :], start=True, stop=True)
                    mm.then_inc(pe_done["mha_t_done"], 1)
                if A:
                    gat_product(1)
                if B:
                    pe.wait_ge(*read("p2_t", it))
                    ps = at("p2_t")
                    pe.wait_ge(dve_done["add2_norm"], n_b)
                    for b in range(G):
                        mm = pe.transpose(ps[:, b * P:(b + 1) * P], add2_p[:, b, :], ident[:])
                    mm.then_inc(pe_done["p2_t_done"], 1)
                if D:
                    qk_product("k", wk_w)
                if B:
                    pe.wait_ge(*read("gat2", it))
                    ps = at("gat2")
                    pe.wait_ge(act_done["p2_t_ready"], n_b)
                    for oc in range(KC):
                        for b in range(G):
                            c = (oc * G + b) * P
                            mm = pe.matmul(ps[:, c:c + P], wh2[:, b, oc * P:(oc + 1) * P], add2_pt[:, b, :],
                                           start=True, stop=True)
                    mm.then_inc(pe_done["gat2_done"], 1)

            iterations(pe, body)

        @block.scalar
        def _(act):
            act.dma_start(a_cols[:], a_heads).then_inc(prepared["heads_t_landed"], 16)
            act.dma_start(adj_s[:], adj).then_inc(prepared["masks_landed"], 16)
            act.dma_start(ident[:], eye).then_inc(prepared["masks_landed"], 16)
            act.dma_start(pick_f, pick).then_inc(prepared["masks_landed"], 16)
            act.dma_start(pick2_f[:], pick2).then_inc(prepared["masks_landed"], 16)
            act.dma_start(ao_cols[:], a_out).then_inc(prepared["out_landed"], 16)

            def body(g, live, it):
                X, A, B, D, C, E = [stage in live for stage in "XABDCE"]
                n_x, n_a, n_b, n_d, n_c, n_e = [g[stage].plus(1).value() for stage in "XABDCE"]
                if it.first(3):
                    act.wait_ge(prepared["b1_ready"], 1)
                if A:
                    for hp in range(HA // 2):
                        act.wait_ge(pe_done[f"add_scores_done_{hp}"], n_a)
                        act.activation(flat(add_p[:, 2 * hp:2 * hp + 2], "h b m"), at(f"add_scores_{hp}")[:], ACT.Copy,
                                       scale=SLOPE).then_inc(act_done[f"slope_{hp}"], 1)
                    act.wait_ge(dve_done["add_sub"], n_a)
                    t = add_p[:].rearrange("p h b m -> p (h b m)")
                    act.activation(t, t, ACT.Exp).then_inc(act_done["add_exp"], 1)
                if D:
                    act.wait_ge(pe_done["ffn1_done"], n_d)
                    for fc in range(KC):
                        a = act.activation(hid[:, fc].rearrange("p b n -> p (b n)"), at("ffn1")[:, fc * F:(fc + 1) * F],
                                           ACT.Relu, bias=b1_c[:, fc:fc + 1])
                    a.then_inc(act_done["hid_ready"], 1)
                    for fc in range(KC):
                        a = act.activation(hid_p[0][:, fc].rearrange("p b n -> p (b n)"), at("ffn1")[:, fc * F:(fc + 1) * F],
                                           ACT.Relu, bias=b1_c[:, fc:fc + 1])
                    a.then_inc(act_done["hid_high"], 1)

                def qk_exp(half):
                    act.wait_ge(dve_done[f"qk_sub_{half}"], n_c)
                    t = qk_p[:, 2 * half:2 * half + 2].rearrange("p r o b m -> p (r o b m)")
                    act.activation(t, t, ACT.Exp, scale=float(DH) ** -0.5).then_inc(act_done[f"qk_exp_{half}"], 1)

                if C:
                    qk_exp(0)
                if D:
                    act.wait_ge(pe_done["h_t_done"], n_d)
                    act.activation(h_res[:].rearrange("p b n -> p (b n)"), at("h_t")[:], ACT.Copy)\
                        .then_inc(act_done["h_t_ready"], 1)
                if C:
                    qk_exp(1)

                def wh_copy(b):
                    act.wait_ge(pe_done[f"wh_done_{b}"], n_a)
                    a = act.activation(wh[:, b, :], at(f"wh_{b}")[:], ACT.Copy, bias=1.0)
                    a.then_inc(act_done[f"wh_ready_{b}"], 1)

                if it.first(1):
                    act.wait_ge(prepared["wh_low"], 1)
                if it.first(2):
                    act.wait_ge(prepared["small_landed"], small_all)
                    for i, (_, pair) in enumerate(small_w):
                        act.activation(pair[0][:], small_stage(i), ACT.Copy).then_inc(prepared["small_high"], 1)

                if A:
                    wh_copy(0)
                    for hp in range(HA // 2):
                        act.wait_ge(pe_done[f"p_t_done_{hp}"], n_a)
                        act.activation(add_pt[:, 2 * hp:2 * hp + 2].rearrange("p h b m -> p (h b m)"),
                                       at(f"p_t_{hp}")[:], ACT.Copy)\
                            .then_inc(act_done[f"p_t_ready_{hp}"], 1)
                    wh_copy(1)

                def qk_probs_copy(half):
                    act.wait_ge(pe_done[f"qk_probs_t_done_{half}"], n_c)
                    act.activation(qk_pt[:, 2 * half:2 * half + 2].rearrange("p r o b m -> p (r o b m)"),
                                   at(f"qk_probs_t_{half}")[:], ACT.Copy).then_inc(act_done[f"qk_pt_ready_{half}"], 1)

                if C:
                    qk_probs_copy(0)
                if X:
                    par = g["X"].base % 2
                    act.wait_ge(x_landed[par], g["X"].half().plus(1).times(16).value())
                    act.activation(x_t[0][:].rearrange("p k b n -> p (k b n)"), x_in[:, par], ACT.Copy)\
                        .then_inc(act_done["x_t_high"], 1)
                if it.first(0):
                    act.wait_ge(prepared["masks_landed"], 16 * 4)
                    act.activation(ident_b[:], ident[:], ACT.Copy).then_inc(prepared["idents_ready"], 1)
                    act.activation(pick_r[:], pick_f, ACT.Copy).then_inc(prepared["idents_ready"], 1)
                    act.activation(pick2_r[:], pick2_f[:], ACT.Copy).then_inc(prepared["idents_ready"], 1)
                    act.wait_ge(prepared["pool_constants"], 5)
                    act.activation(ones_r[:], ones, ACT.Copy).then_inc(prepared["idents_ready"], 1)
                    act.wait_ge(prepared["heads_landed"], 16 * KC)
                    act.activation(flat(wh_w[0][:], "k n"), stage_w, ACT.Copy).then_inc(prepared["wh_high"], 1)
                if C:
                    act.wait_ge(pe_done["v_done"], n_c)
                    act.activation(v_s[:].rearrange("p b h d -> p (b h d)"), at("v")[:], ACT.Copy)\
                        .then_inc(act_done["v_ready"], 1)
                if D:
                    act.wait_ge(pe_done["x1_t_done"], n_d)
                    act.activation(x1_t[0][:].rearrange("p k b n -> p (k b n)"), at("x1_t")[:], ACT.Copy)\
                        .then_inc(act_done["x1_t_high"], 1)
                if B:
                    act.wait_ge(pe_done["add2_scores_done"], n_b)
                    act.activation(flat(add2_p[:], "b m"), at("add2_scores")[:, 0:G * P], ACT.Copy, scale=SLOPE)\
                        .then_inc(act_done["slope2"], 1)
                if A:
                    act.wait_ge(pe_done["gat_done_0"], n_a)
                    act.activation(gat_e[:, 0, :], at("gat_0")[:], ACT.Exp, bias=-1.0).then_inc(act_done["gat_exp_0"], 1)
                if it.first(1):
                    act.wait_ge(prepared["out_scores_copied"], 1)
                    act.activation(wo_w[0][:], stage_wo, ACT.Copy).then_inc(prepared["wo_high"], 1)
                if C:
                    qk_probs_copy(1)
                if X:
                    act.wait_ge(pe_done["f_t_done"], n_x)
                    act.activation(f_t[:].rearrange("p b n -> p (b n)"), at("f_t")[0:LOW + 2 * HA, 0:G * P], ACT.Copy)\
                        .then_inc(act_done["f_t_high"], 1)
                if B:
                    act.wait_ge(dve_done["add2_sub"], n_b)
                    t = add2_p[:].rearrange("p b m -> p (b m)")
                    act.activation(t, t, ACT.Exp).then_inc(act_done["add2_exp"], 1)
                if A:
                    act.wait_ge(dve_done["gat_ready_0"], n_a)
                    act.activation(flat(gat_gp[0][:, 0], "k n"), gat_g[:, 0], ACT.Copy).then_inc(act_done["gat_high_0"], 1)

                def add_bias(name, dst, bias):
                    act.wait_ge(pe_done[f"{name}_done"], n_d)
                    for ob in range(OB):
                        a = act.activation(dst[:, ob].rearrange("p b n -> p (b n)"), at(name)[:, ob * F:(ob + 1) * F],
                                           ACT.Identity, bias=bias[:, ob:ob + 1])
                    a.then_inc(act_done[f"{name}_ready"], 1)

                if D:
                    add_bias("q", q_s, bq_c)
                if C:
                    act.wait_ge(pe_done["mha_t_done"], n_c)
                    for ob in range(OB):
                        a = act.activation(mha_t[0][:, ob].rearrange("p b n -> p (b n)"), at("mha_t")[:, ob * F:(ob + 1) * F],
                                           ACT.Identity, bias=bv_c[:, ob:ob + 1])
                    a.then_inc(act_done["mha_t_high"], 1)
                if A:
                    act.wait_ge(pe_done["gat_done_1"], n_a)
                    act.activation(gat_e[:, 1, :], at("gat_1")[:], ACT.Exp, bias=-1.0).then_inc(act_done["gat_exp_1"], 1)
                if B:
                    act.wait_ge(pe_done["p2_t_done"], n_b)
                    act.activation(add2_pt[:].rearrange("p b n -> p (b n)"), at("p2_t")[:, 0:G * P], ACT.Copy)\
                        .then_inc(act_done["p2_t_ready"], 1)
                if D:
                    add_bias("k", k_s, bk_c)
                if B:
                    act.wait_ge(pe_done["gat2_done"], n_b)
                    act.activation(gat2_e.rearrange("p k b n -> p (k b n)"), at("gat2")[:], ACT.Exp,
                                   bias=-1.0).then_inc(act_done["gat2_exp"], 1)
                if E:
                    par = g["E"].base % 2
                    act.wait_ge(pool_done["shift2_ready"], n_e)
                    if g["E"].base >= 2:
                        act.wait_ge(stored[par], g["E"].half().times(16).value())
                    for b in range(G):
                        a = act.activation(out_s[:, par, b], y2[:, par, b], ACT.Identity, bias=shift2[:, b:b + 1],
                                           scale=rstd2[:, b:b + 1])
                    a.then_inc(act_done["out_ready"], 1)
                if B:
                    act.wait_ge(dve_done["gat2_ready"], n_b)
                    act.activation(gat2_gp[0][:], gat2_g, ACT.Copy).then_inc(act_done["gat2_high"], 1)

            iterations(act, body)

        @block.gpsimd
        def _(pool):
            pool.memset(stage_f[:], 0.0).then_inc(prepared["pool_constants"], 1)
            pool.memset(ones, 1.0).then_inc(prepared["pool_constants"], 1)
            pool.memset(power[:], -0.5).then_inc(prepared["pool_constants"], 1)
            pool.memset(eps[:], EPS).then_inc(prepared["pool_constants"], 1)
            pool.memset(zero[:], 0.0).then_inc(prepared["pool_constants"], 1)
            pool.wait_ge(prepared["wh_high"], 1)
            pool.tensor_tensor(flat(wh_w[1][:], "k n"), stage_w, flat(wh_w[0][:], "k n").bitcast(F32), ALU.subtract)\
                .then_inc(prepared["wh_low"], 1)
            pool.wait_ge(prepared["pool_constants"], 5)

            def inverse_deviation(var, vare, var_ready, vare_ready, rstd, rstd_ready, n):
                pool.wait_ge(var_ready, n)
                pool.tensor_tensor(vare[:], var, eps[:], ALU.add).then_inc(vare_ready, 1)
                pool.wait_ge(vare_ready, n)
                pool.tensor_tensor(rstd[:], vare[:], power[:], ALU.pow).then_inc(rstd_ready, 1)

            def body(g, live, it):
                A, D, C, E = ("A" in live), ("D" in live), ("C" in live), ("E" in live)
                n_a, n_d, n_c, n_e = [g[stage].plus(1).value() for stage in "ADCE"]
                if it.first(2):
                    for i, (_, pair) in enumerate(small_w):
                        pool.wait_ge(prepared["small_high"], i + 1)
                        pool.tensor_tensor(pair[1][:], small_stage(i), pair[0][:].bitcast(F32), ALU.subtract)\
                            .then_inc(prepared["small_low"], 1)
                if it.first(3):
                    pool.wait_ge(prepared["b1_ready"], 1)

                def qk_normalise(half):
                    pool.wait_ge(act_done[f"qk_exp_{half}"], n_c)
                    pool.wait_ge(dve_done[f"qk_rec_ready_{half}"], n_c)
                    t = qk_p[:, 2 * half:2 * half + 2].rearrange("p r o b m -> p (r o b) m")
                    rec = flat(qk_rec[:, 2 * half:2 * half + 2], "r j")
                    pool.tensor_tensor(t, t, rec.unsqueeze(2).broadcast_to([P, 2 * OB * G, P]), ALU.mult)\
                        .then_inc(pool_done[f"qk_norm_{half}"], 1)

                if D:
                    par = g["D"].base % 2
                    pool.wait_ge(xres_landed[par], g["D"].half().plus(1).times(16).value())
                    for b in range(G):
                        p = pool.tensor_tensor(xb[:, b], x_res[:, par, b], beta_r[:], ALU.add)
                    p.then_inc(pool_done["xb_ready"], 1)
                    pool.wait_ge(act_done["h_t_ready"], n_d)
                    for b in range(G):
                        p = pool.tensor_tensor(h_res[:, b], h_res[:, b], b2_r[:], ALU.add)
                    p.then_inc(pool_done["h_ready"], 1)
                    inverse_deviation(mv[:, :, 1], vare, dve_done["y_mv"], pool_done["vare_ready"], rstd,
                                      pool_done["rstd_ready"], n_d)
                if C:
                    qk_normalise(0)
                if D:
                    inverse_deviation(mv1[:, :, 1], vare1, dve_done["y1_mv"], pool_done["vare1_ready"], rstd1,
                                      pool_done["rstd1_ready"], n_d)
                if C:
                    qk_normalise(1)
                if D:
                    par = g["D"].base % 2
                    pool.wait_ge(dve_done["x1_ready"], n_d)
                    for b in range(G):
                        p = pool.tensor_tensor(x1b[:, par, b], x1[:, b], bo_r[:], ALU.add)
                    p.then_inc(pool_done["x1b_ready"], 1)
                if E:
                    if g["E"].base >= 1:
                        pool.wait_ge(act_done["out_ready"], g["E"].value())
                    inverse_deviation(mv2[:, g["E"].base % 2, :, 1], vare2, dve_done["y2_mv"], pool_done["vare2_ready"],
                                      rstd2, pool_done["rstd2_ready"], n_e)
                    pool.tensor_tensor(minus_mean2[:], zero[:], mv2[:, g["E"].base % 2, :, 0], ALU.subtract)\
                        .then_inc(pool_done["minus_mean2"], 1)
                    pool.wait_ge(pool_done["minus_mean2"], n_e)
                    pool.wait_ge(pool_done["rstd2_ready"], n_e)
                    pool.tensor_tensor(shift2[:], minus_mean2[:], rstd2[:], ALU.mult).then_inc(pool_done["shift2_ready"], 1)
                if A:
                    for b in range(G):
                        pool.wait_ge(gat_high[b], n_a)
                        pool.tensor_tensor(gat_gp[1][:, b].rearrange("p k n -> p (k n)"), gat_g[:, b, :],
                                           gat_gp[0][:, b].rearrange("p k n -> p (k n)").bitcast(F32), ALU.subtract)\
                            .then_inc(pool_done[f"gat_low_{b}"], 1)

            iterations(pool, body)

        @block.vector
        def _(dve):
            dve.wait_ge(prepared["pool_constants"], 5)
            dve.wait_ge(prepared["head_scores"], 1)
            scores = bank["b7"][:, 0:KC * HA * 2].rearrange("p (k h t) -> p k h t", k=KC, h=HA)
            for c in (0, LOW):
                dve.tensor_copy(stage_f[:, :, c:c + 2 * HA].rearrange("p k (t h) -> p k h t", h=HA), scores)\
                    .then_inc(prepared["head_scores_copied"], 1)
            dve.wait_ge(prepared["head_scores_copied"], 2)
            dve.tensor_copy(wf_w[0][:], stage_f[:]).then_inc(prepared["wf_high"], 1)
            dve.wait_ge(prepared["wf_high"], 1)
            dve.tensor_tensor(wf_w[1][:], stage_f[:], wf_w[0][:].bitcast(F32), ALU.subtract)\
                .then_inc(prepared["wf_parts"], 1)
            dve.wait_ge(prepared["masks_landed"], 16 * 4)
            dve.tensor_scalar(mask4[:], adj_s[:].unsqueeze(1).broadcast_to([P, 4, P]), 0, MASKED, ALU.is_le, ALU.mult)\
                .then_inc(prepared["mask_ready"], 1)

            def row_stats(src, stats, ready):
                for b in range(G):
                    d = dve.bn_stats(stats[:, b], src[:, b])
                d.then_inc(ready, 1)

            def mean_variance(mv, stats, ready):
                for b in range(G):
                    d = dve.bn_aggr(mv[:, b], stats[:, b])
                d.then_inc(ready, 1)

            def body(g, live, it):
                X, A, B, D, C, E = [stage in live for stage in "XABDCE"]
                n_x, n_a, n_b, n_d, n_c, n_e = [g[stage].plus(1).value() for stage in "XABDCE"]
                if it.first(1):
                    dve.wait_ge(prepared["idents_ready"], 2)
                if it.first(2):
                    dve.wait_ge(prepared["sums_done"], 1)
                    dve.tensor_scalar(colsum[:, 0:F], bank["d1"][:, 0:F], -1.0, None, ALU.add)
                    dve.tensor_copy(colsum[:, F:F + 2], bank["d1"][:, F:F + 2])
                    dve.wait_ge(prepared["sums_done"], 2)
                    dve.tensor_scalar(b2_r[:], b2_r[:], -1.0, None, ALU.add)
                    dve.tensor_tensor(b1_c[:], b1_c[:], bank["d1"][:, 512:512 + KC], ALU.subtract)\
                        .then_inc(prepared["b1_ready"], 1)
                    dve.wait_ge(prepared["b1_ready"], 1)
                if A:
                    for hp in range(HA // 2):
                        dve.wait_ge(act_done[f"slope_{hp}"], n_a)
                        p2 = flat(add_p[:, 2 * hp:2 * hp + 2], "h b m")
                        dve.tensor_tensor(p2, at(f"add_scores_{hp}")[:], p2, ALU.max)\
                            .then_inc(dve_done[f"leaky_{hp}"], 1)
                    dve.wait_ge(dve_done["leaky_1"], n_a)
                    p3 = add_p[:].rearrange("p h b m -> p (h b) m")
                    dve.tensor_reduce(add_max[:], p3, AX, ALU.max).then_inc(dve_done["add_max_ready"], 1)
                    dve.wait_ge(dve_done["add_max_ready"], n_a)
                    dve.tensor_tensor(p3, p3, add_max[:].unsqueeze(2).broadcast_to([P, HA * G, P]), ALU.subtract)\
                        .then_inc(dve_done["add_sub"], 1)

                def qk_less_max(half):
                    dve.wait_ge(pe_done[f"qk_scores_done_{half}"], n_c)
                    s3 = at(f"qk_scores_{half}")[:].rearrange("p (j m) -> p j m", m=P)
                    mx = flat(qk_max[:, 2 * half:2 * half + 2], "r j")
                    dve.tensor_reduce(mx, s3, AX, ALU.max).then_inc(dve_done[f"qk_max_{half}"], 1)
                    dve.wait_ge(dve_done[f"qk_max_{half}"], n_c)
                    dve.tensor_tensor(qk_p[:, 2 * half:2 * half + 2].rearrange("p r o b m -> p (r o b) m"), s3,
                                      mx.unsqueeze(2).broadcast_to([P, 2 * OB * G, P]), ALU.subtract)\
                        .then_inc(dve_done[f"qk_sub_{half}"], 1)

                if C:
                    qk_less_max(0)
                if E:
                    par = g["E"].base % 2
                    dve.wait_ge(pe_done["proj_done"], n_e)
                    dve.wait_ge(pool_done["x1b_ready"], n_e)
                    dve.tensor_tensor(y2[:, par], at("proj")[:].rearrange("p (b n) -> p b n", b=G), x1b[:, par],
                                      ALU.add).then_inc(dve_done["y2_ready"], 1)
                    dve.wait_ge(dve_done["y2_ready"], n_e)
                    row_stats(y2[:, par], stats2, dve_done["y2_stats"])
                if D:
                    dve.wait_ge(act_done["hid_high"], n_d)
                    dve.tensor_tensor(flat(hid_p[1][:], "k b n"), flat(hid[:], "k b n"),
                                      flat(hid_p[0][:], "k b n").bitcast(F32), ALU.subtract).then_inc(dve_done["hid_low"], 1)
                if A:
                    dve.wait_ge(act_done["add_exp"], n_a)
                    p3 = add_p[:].rearrange("p h b m -> p (h b) m")
                    dve.tensor_reduce(add_sum[:], p3, AX, ALU.add).then_inc(dve_done["add_sum_ready"], 1)

                def qk_sums(half):
                    dve.wait_ge(act_done[f"qk_exp_{half}"], n_c)
                    t = qk_p[:, 2 * half:2 * half + 2].rearrange("p r o b m -> p (r o b) m")
                    dve.tensor_reduce(flat(qk_sum[:, 2 * half:2 * half + 2], "r j"), t, AX, ALU.add)\
                        .then_inc(dve_done[f"qk_sum_ready_{half}"], 1)
                    dve.wait_ge(dve_done[f"qk_sum_ready_{half}"], n_c)
                    dve.reciprocal(flat(qk_rec[:, 2 * half:2 * half + 2], "r j"),
                                   flat(qk_sum[:, 2 * half:2 * half + 2], "r j"))\
                        .then_inc(dve_done[f"qk_rec_ready_{half}"], 1)

                if C:
                    qk_less_max(1)
                if D:
                    dve.wait_ge(pe_done["ffn2_done"], n_d)
                    dve.wait_ge(pool_done["h_ready"], n_d)
                    dve.tensor_tensor(y[:], at("ffn2")[:].rearrange("p (b n) -> p b n", b=G), h_res[:], ALU.add)\
                        .then_inc(dve_done["y_ready"], 1)
                    dve.wait_ge(dve_done["y_ready"], n_d)
                    row_stats(y, stats, dve_done["y_stats"])
                    dve.wait_ge(dve_done["y_stats"], n_d)
                if A:
                    dve.wait_ge(dve_done["add_sum_ready"], n_a)
                    dve.reciprocal(add_rec[:], add_sum[:]).then_inc(dve_done["add_rec_ready"], 1)
                if D:
                    mean_variance(mv, stats, dve_done["y_mv"])
                if A:
                    dve.wait_ge(dve_done["add_rec_ready"], n_a)
                    dve.tensor_tensor(p3, p3, add_rec[:].unsqueeze(2).broadcast_to([P, HA * G, P]), ALU.mult)\
                        .then_inc(dve_done["add_norm"], 1)
                def wh2_values(b):
                    dve.wait_ge(pe_done[f"wh2_done_{b}"], n_b)
                    dve.tensor_tensor(wh2[:, b], at(f"wh2_{b}")[:, 0:F + 2], colsum[:], ALU.subtract)\
                        .then_inc(dve_done[f"wh2_ready_{b}"], 1)

                if B:
                    wh2_values(0)
                if C:
                    qk_sums(0)
                if D:
                    dve.wait_ge(pool_done["rstd_ready"], n_d)
                    for b in range(G):
                        d = dve.scalar_tensor_tensor(out=y[:, b], in0=y[:, b], scalar=mv[:, b, 0:1], in1=gamma_r[:],
                                                     op0=ALU.subtract, op1=ALU.mult)
                    d.then_inc(dve_done["y_scaled"], 1)
                    dve.wait_ge(dve_done["y_scaled"], n_d)
                    for b in range(G):
                        d = dve.scalar_tensor_tensor(out=y[:, b], in0=y[:, b], scalar=rstd[:, b:b + 1], in1=xb[:, b],
                                                     op0=ALU.mult, op1=ALU.add)
                    d.then_inc(dve_done["y_added"], 1)
                    dve.wait_ge(dve_done["y_added"], n_d)
                    row_stats(y, stats1, dve_done["y1_stats"])
                    dve.wait_ge(dve_done["y1_stats"], n_d)
                if B:
                    wh2_values(1)
                if D:
                    mean_variance(mv1, stats1, dve_done["y1_mv"])
                if B:
                    dve.wait_ge(dve_done["wh2_ready_1"], n_b)
                    dve.tensor_copy(f2[:, :, 0:2].bitcast(F32R), wh2[:, :, F:F + 2]).then_inc(dve_done["f2_high"], 1)
                    dve.wait_ge(dve_done["f2_high"], n_b)
                    dve.tensor_tensor(f2[:, :, 2:4], wh2[:, :, F:F + 2], f2[:, :, 0:2], ALU.subtract)\
                        .then_inc(dve_done["f2_low"], 1)
                if E:
                    dve.wait_ge(dve_done["y2_stats"], n_e)
                if C:
                    qk_sums(1)
                if E:
                    mean_variance(mv2[:, g["E"].base % 2], stats2, dve_done["y2_mv"])
                if D:
                    dve.wait_ge(pool_done["rstd1_ready"], n_d)
                    for b in range(G):
                        d = dve.tensor_scalar(x1[:, b], y[:, b], mv1[:, b, 0:1], rstd1[:, b:b + 1],
                                              ALU.subtract, ALU.mult)
                    d.then_inc(dve_done["x1_ready"], 1)
                if B:
                    dve.wait_ge(pe_done["f2_t_done"], n_b)
                    dve.tensor_copy(flat(f2_t[:], "b n"), at("f2_t")[0:4, 0:G * P]).then_inc(dve_done["f2_t_ready"], 1)
                if X:
                    dve.wait_ge(act_done["x_t_high"], n_x)
                    dve.tensor_tensor(flat(x_t[1][:], "k b n"), x_in[:, g["X"].base % 2], flat(x_t[0][:], "k b n").bitcast(F32),
                                      ALU.subtract).then_inc(dve_done["x_t_low"], 1)
                if D:
                    dve.wait_ge(act_done["x1_t_high"], n_d)
                    dve.tensor_tensor(flat(x1_t[1][:], "k b n"), at("x1_t")[:], flat(x1_t[0][:], "k b n").bitcast(F32),
                                      ALU.subtract).then_inc(dve_done["x1_t_low"], 1)
                if B:
                    dve.wait_ge(act_done["slope2"], n_b)
                    p2 = flat(add2_p[:], "b m")
                    dve.tensor_tensor(p2, at("add2_scores")[:, 0:G * P], p2, ALU.max).then_inc(dve_done["leaky2"], 1)
                    dve.wait_ge(dve_done["leaky2"], n_b)
                    dve.tensor_reduce(add2_max[:], add2_p[:], AX, ALU.max).then_inc(dve_done["add2_max_ready"], 1)
                    dve.wait_ge(dve_done["add2_max_ready"], n_b)
                    dve.tensor_tensor(add2_p[:], add2_p[:], add2_max[:].unsqueeze(2).broadcast_to([P, G, P]),
                                      ALU.subtract).then_inc(dve_done["add2_sub"], 1)

                def gat(b):
                    dve.wait_ge(act_done[f"gat_exp_{b}"], n_a)
                    dve.scalar_tensor_tensor(out=gat_g[:, b], in0=gat_e[:, b], scalar=1.0, in1=at(f"gat_{b}")[:],
                                             op0=ALU.min, op1=ALU.max).then_inc(dve_done[f"gat_ready_{b}"], 1)

                if A:
                    gat(0)
                if it.first(1):
                    dve.wait_ge(prepared["out_scores"], 1)
                    dve.tensor_copy(stage_wo[:, :, F:F + 2], bank["b6"][:, 0:2 * K1].rearrange("p (k t) -> p k t", k=K1))\
                        .then_inc(prepared["out_scores_copied"], 1)
                    dve.wait_ge(prepared["wo_high"], 1)
                    dve.tensor_tensor(wo_w[1][:], stage_wo, wo_w[0][:].bitcast(F32), ALU.subtract)\
                        .then_inc(prepared["wo_parts"], 1)
                if B:
                    dve.wait_ge(act_done["add2_exp"], n_b)
                    dve.tensor_reduce(add2_sum[:], add2_p[:], AX, ALU.add).then_inc(dve_done["add2_sum_ready"], 1)
                    dve.wait_ge(dve_done["add2_sum_ready"], n_b)
                    dve.reciprocal(add2_rec[:], add2_sum[:]).then_inc(dve_done["add2_rec_ready"], 1)
                    dve.wait_ge(dve_done["add2_rec_ready"], n_b)
                    dve.tensor_tensor(add2_p[:], add2_p[:], add2_rec[:].unsqueeze(2).broadcast_to([P, G, P]),
                                      ALU.mult).then_inc(dve_done["add2_norm"], 1)
                if X:
                    dve.wait_ge(act_done["f_t_high"], n_x)
                    low = flat(f_t[LOW:LOW + 2 * HA], "b n")
                    dve.tensor_tensor(low, at("f_t")[LOW:LOW + 2 * HA, 0:G * P], low.bitcast(F32), ALU.subtract)\
                        .then_inc(dve_done["f_t_low"], 1)
                if C:
                    dve.wait_ge(act_done["mha_t_high"], n_c)
                    for ob in range(OB):
                        d = dve.scalar_tensor_tensor(out=flat(mha_t[1][:, ob], "b n"), in0=at("mha_t")[:, ob * F:(ob + 1) * F],
                                                     scalar=bv_c[:, ob:ob + 1], in1=flat(mha_t[0][:, ob], "b n").bitcast(F32),
                                                     op0=ALU.add, op1=ALU.subtract)
                    d.then_inc(dve_done["mha_t_low"], 1)
                if A:
                    gat(1)
                    dve.wait_ge(dve_done["gat_ready_1"], n_a)
                    dve.tensor_copy(flat(gat_gp[0][:, 1], "k n"), gat_g[:, 1]).then_inc(dve_done["gat_high_1"], 1)
                if B:
                    dve.wait_ge(act_done["gat2_exp"], n_b)
                    dve.scalar_tensor_tensor(out=flat(gat2_g, "k b n"), in0=flat(gat2_e, "k b n"), scalar=1.0,
                                             in1=at("gat2")[:], op0=ALU.min, op1=ALU.max).then_inc(dve_done["gat2_ready"], 1)
                    dve.wait_ge(act_done["gat2_high"], n_b)
                    dve.tensor_tensor(flat(gat2_gp[1][:], "k b n"), flat(gat2_g, "k b n"),
                                      flat(gat2_gp[0][:], "k b n").bitcast(F32), ALU.subtract).then_inc(dve_done["gat2_low"], 1)

            iterations(dve, body)


def kernel(x, adj, L0_gnn_W_heads, L0_gnn_a_heads, L0_gnn_W_out, L0_gnn_a_out, L0_gnn_w1, L0_gnn_b1, L0_gnn_w2,
           L0_gnn_b2, L0_gnn_ln_gamma, L0_gnn_ln_beta, L1_gnn_Wq, L1_gnn_bq, L1_gnn_Wk, L1_gnn_bk, L1_gnn_Wv,
           L1_gnn_bv, L1_gnn_Wo, L1_gnn_bo):
    import numpy as np
    import concourse.bacc as bacc
    from concourse.bass_utils import run_bass_kernel_spmd

    pick = np.zeros((LOW + 2 * HA, 2 * HA, P), np.float32)
    for c in range(2 * HA):
        pick[[c, LOW + c], c] = 1.0
    pick2 = np.zeros((4, 2, P), np.float32)
    for c in range(2):
        pick2[[c, 2 + c], c] = 1.0

    def columns(v):
        return np.asarray(v).reshape(-1, P).T

    x_t = np.asarray(x).reshape(-1, G, P, KC, P).transpose(4, 0, 3, 1, 2).reshape(P, -1, KC * G * P)
    w_heads_t = np.asarray(L0_gnn_W_heads).reshape(HA, F, KC, P).transpose(3, 0, 2, 1)
    arrays = {
        "x": x, "xT": x_t, "adj": adj, "W_heads": L0_gnn_W_heads, "W_headsT": w_heads_t,
        "a_heads": np.asarray(L0_gnn_a_heads).reshape(HA, 2, KC, P).transpose(3, 0, 2, 1), "W_out": L0_gnn_W_out,
        "W_outT": np.asarray(L0_gnn_W_out).reshape(K1 * P, KC, P).transpose(2, 1, 0),
        "a_out": np.asarray(L0_gnn_a_out).reshape(2, KC, P).transpose(2, 1, 0),
        "w1": L0_gnn_w1, "b1": columns(L0_gnn_b1), "w2": L0_gnn_w2, "b2": L0_gnn_b2,
        "ln_gamma": L0_gnn_ln_gamma, "ln_beta": L0_gnn_ln_beta,
        "WqT": np.asarray(L1_gnn_Wq).T, "bq": columns(L1_gnn_bq), "WkT": np.asarray(L1_gnn_Wk).T, "bk": columns(L1_gnn_bk),
        "WvT": np.asarray(L1_gnn_Wv).T, "bv": columns(L1_gnn_bv), "WoT": np.asarray(L1_gnn_Wo).T, "bo": L1_gnn_bo,
        "eye": np.eye(P, dtype=np.float32), "pick": pick, "pick2": pick2,
    }
    nc = bacc.Bacc("TRN2", target_bir_lowering=False, num_devices=1)
    feeds, args = {}, {}
    for name, a in arrays.items():
        a = np.ascontiguousarray(a)
        feeds[f"in_{name}"] = a
        args[name] = nc.dram_tensor(f"in_{name}", a.shape, mybir.dt.from_np(a.dtype), kind="ExternalInput").ap()
    out = nc.dram_tensor("out_x", tuple(np.shape(x)), F32, kind="ExternalOutput").ap()
    build(nc, out=out, **args)
    return run_bass_kernel_spmd(nc, [feeds], core_ids=[0]).results[0]["out_x"]
```
